# Optimizing a Trainium2 kernel written in Bass

```python
import numpy as np
import jax
import jax.numpy as jnp

def _softmax(x, axis=-1):
    return jax.nn.softmax(x, axis=axis)

def _gelu(x):
    return jax.nn.gelu(x, approximate=True)

def _silu(x):
    return jax.nn.silu(x)

def _sigmoid(x):
    return jax.nn.sigmoid(x)

def _layernorm(x, axis=-1, eps=1e-05):
    m = jnp.mean(x, axis=axis, keepdims=True)
    v = jnp.var(x, axis=axis, keepdims=True)
    return (x - m) / jnp.sqrt(v + eps)

def _scatter_add(tgt, idx, src, axis=0):
    return tgt.at[idx].add(src)

def _segment_sum(src, seg, n):
    return jax.ops.segment_sum(src, seg, n)
kernel_name = 'mk_adj_resnorm_d2_adj_r2_b9a0ea'

def setup_inputs(seed: int=0):
    np.random.seed(seed)
    _w = jnp.asarray

    def _rec_inputs():
        import jax
        import jax.numpy as jnp
        _gk = jax.random.key(seed)
        x = 7.22e-05 + 1 * jax.random.normal(jax.random.fold_in(_gk, 1), (64, 128, 256), jnp.float32)
        _a = jax.random.bernoulli(jax.random.fold_in(_gk, 2), 0.03125, (64, 128, 128))
        _a = jnp.logical_or(_a, jnp.swapaxes(_a, -1, -2))
        _a = jnp.logical_or(_a, jnp.eye(128, dtype=bool))
        _af = _a.astype(jnp.float32)
        _af = _af * jax.random.uniform(jax.random.fold_in(_gk, 3), (64, 128, 128), jnp.float32, 0.05, 1)
        adj = _af
        return (x, adj)
    x, adj = _rec_inputs()

    def _L0_gnn_setup():
        import jax, jax.numpy as jnp
        import numpy as np
        EPS_LN = 1e-05

        def hypergraph_conv(x, adj, W, b):
            N, C, _ = adj.shape
            H = (adj != 0).astype(x.dtype)
            w = adj.reshape(N, -1)[:, :C]
            xw = jnp.einsum('ncd,hd->nch', x, W)
            Dn = jnp.einsum('nce,ne->nc', H, w)
            Dn = jnp.where(Dn > 0, 1.0 / Dn, 0.0)
            Be = H.sum(axis=1)
            Be = jnp.where(Be > 0, 1.0 / Be, 0.0)
            m = Be[:, :, None] * jnp.einsum('nce,nch->neh', H, xw)
            out = Dn[:, :, None] * jnp.einsum('nce,neh->nch', H, m)
            return out + b

        def layer_norm(x, g, b):
            mu = jnp.mean(x, axis=-1, keepdims=True)
            var = jnp.var(x, axis=-1, keepdims=True)
            return (x - mu) * jax.lax.rsqrt(var + EPS_LN) * g + b
        key = jax.random.key(seed)
        ks = jax.random.split(key, 4)
        N, C, Din, Dh, Dout = (16, 512, 256, 512, 256)
        x = jax.random.normal(ks[0], (N, C, Din), dtype=jnp.float32)
        adj = jax.random.uniform(ks[1], (N, C, C), dtype=jnp.float32, minval=0.1, maxval=1.0)
        W1 = jax.random.normal(ks[2], (Dh, Din), dtype=jnp.float32) * (1.0 / np.sqrt(Din))
        b1 = jnp.zeros((Dh,), dtype=jnp.float32)
        gamma = jnp.ones((Dh,), dtype=jnp.float32)
        beta = jnp.zeros((Dh,), dtype=jnp.float32)
        W2 = jax.random.normal(ks[3], (Dout, Dh), dtype=jnp.float32) * (1.0 / np.sqrt(Dh))
        b2 = jnp.zeros((Dout,), dtype=jnp.float32)
        return {'x': x, 'adj': adj, 'W1': W1, 'b1': b1, 'gamma': gamma, 'beta': beta, 'W2': W2, 'b2': b2}
    _L0_gnn_all = _L0_gnn_setup()
    _L0_gnn_in = {k: v for k, v in _L0_gnn_all.items() if k in ('W1', 'b1', 'gamma', 'beta', 'W2', 'b2')}
    del _L0_gnn_all

    def _L1_gnn_setup():
        import jax, jax.numpy as jnp
        import numpy as np
        B, N, D = (8, 1024, 256)
        key = jax.random.key(seed)
        ks = jax.random.split(key, 8)
        scale = 0.5 / np.sqrt(D)
        x = jax.random.normal(ks[0], (B, N, D), dtype=jnp.float32)
        adj = jax.random.uniform(ks[1], (B, N, N), dtype=jnp.float32)
        Wq_w = jax.random.normal(ks[2], (D, D), dtype=jnp.float32) * scale
        Wk_w = jax.random.normal(ks[3], (D, D), dtype=jnp.float32) * scale
        Wv_w = jax.random.normal(ks[4], (D, D), dtype=jnp.float32) * scale
        Wq_b = jnp.zeros((D,), dtype=jnp.float32)
        Wk_b = jnp.zeros((D,), dtype=jnp.float32)
        Wv_b = jnp.zeros((D,), dtype=jnp.float32)
        return {'x': x, 'adj': adj, 'Wq_w': Wq_w, 'Wq_b': Wq_b, 'Wk_w': Wk_w, 'Wk_b': Wk_b, 'Wv_w': Wv_w, 'Wv_b': Wv_b}
    _L1_gnn_all = _L1_gnn_setup()
    _L1_gnn_in = {k: v for k, v in _L1_gnn_all.items() if k in ('Wq_w', 'Wq_b', 'Wk_w', 'Wk_b', 'Wv_w', 'Wv_b')}
    del _L1_gnn_all
    return {'x': x, 'adj': adj, 'L0_gnn_W1': _L0_gnn_in['W1'], 'L0_gnn_b1': _L0_gnn_in['b1'], 'L0_gnn_gamma': _L0_gnn_in['gamma'], 'L0_gnn_beta': _L0_gnn_in['beta'], 'L0_gnn_W2': _L0_gnn_in['W2'], 'L0_gnn_b2': _L0_gnn_in['b2'], 'L1_gnn_Wq_w': _L1_gnn_in['Wq_w'], 'L1_gnn_Wq_b': _L1_gnn_in['Wq_b'], 'L1_gnn_Wk_w': _L1_gnn_in['Wk_w'], 'L1_gnn_Wk_b': _L1_gnn_in['Wk_b'], 'L1_gnn_Wv_w': _L1_gnn_in['Wv_w'], 'L1_gnn_Wv_b': _L1_gnn_in['Wv_b']}

def reference(x, adj, L0_gnn_W1, L0_gnn_b1, L0_gnn_gamma, L0_gnn_beta, L0_gnn_W2, L0_gnn_b2, L1_gnn_Wq_w, L1_gnn_Wq_b, L1_gnn_Wk_w, L1_gnn_Wk_b, L1_gnn_Wv_w, L1_gnn_Wv_b):
    import jax
    import jax.numpy as jnp

    def _L0_gnn_ref(x, adj, W1, b1, gamma, beta, W2, b2):
        import jax, jax.numpy as jnp
        import numpy as np
        EPS_LN = 1e-05

        def hypergraph_conv(x, adj, W, b):
            N, C, _ = adj.shape
            H = (adj != 0).astype(x.dtype)
            w = adj.reshape(N, -1)[:, :C]
            xw = jnp.einsum('ncd,hd->nch', x, W)
            Dn = jnp.einsum('nce,ne->nc', H, w)
            Dn = jnp.where(Dn > 0, 1.0 / Dn, 0.0)
            Be = H.sum(axis=1)
            Be = jnp.where(Be > 0, 1.0 / Be, 0.0)
            m = Be[:, :, None] * jnp.einsum('nce,nch->neh', H, xw)
            out = Dn[:, :, None] * jnp.einsum('nce,neh->nch', H, m)
            return out + b

        def layer_norm(x, g, b):
            mu = jnp.mean(x, axis=-1, keepdims=True)
            var = jnp.var(x, axis=-1, keepdims=True)
            return (x - mu) * jax.lax.rsqrt(var + EPS_LN) * g + b
        h = jax.nn.relu(hypergraph_conv(x, adj, W1, b1))
        h = layer_norm(h, gamma, beta)
        y = hypergraph_conv(h, adj, W2, b2)
        return y + x

    def _L1_gnn_ref(x, adj, Wq_w, Wq_b, Wk_w, Wk_b, Wv_w, Wv_b):
        import jax, jax.numpy as jnp
        import numpy as np
        B, N, D = (8, 1024, 256)
        query = jnp.einsum('bnd,od->bno', x, Wq_w) + Wq_b
        keyt = jnp.einsum('bnd,od->bno', x, Wk_w) + Wk_b
        value = jnp.einsum('bnd,od->bno', x, Wv_w) + Wv_b
        weight = jnp.einsum('bqd,bkd->bqk', query, keyt)
        weight = adj * jnp.exp(weight)
        weight = weight / jnp.sum(weight, axis=2, keepdims=True)
        return jnp.einsum('bqk,bkd->bqd', weight, value)
    x = _layernorm(x + _L0_gnn_ref(x, adj, L0_gnn_W1, L0_gnn_b1, L0_gnn_gamma, L0_gnn_beta, L0_gnn_W2, L0_gnn_b2), axis=-1)
    x = _layernorm(x + _L1_gnn_ref(x, adj, L1_gnn_Wq_w, L1_gnn_Wq_b, L1_gnn_Wk_w, L1_gnn_Wk_b, L1_gnn_Wv_w, L1_gnn_Wv_b), axis=-1)
    return x

_drawn_inputs = setup_inputs


def setup_inputs(seed=0):
    import zlib

    import numpy as np

    out = dict(_drawn_inputs(seed))
    spreads = {'L0_gnn_b1': (0.0, 0.1),
     'L0_gnn_gamma': (1.0, 0.2),
     'L0_gnn_beta': (0.0, 0.1),
     'L0_gnn_b2': (0.0, 0.1),
     'L1_gnn_Wq_b': (0.0, 0.1),
     'L1_gnn_Wk_b': (0.0, 0.1),
     'L1_gnn_Wv_b': (0.0, 0.1)}
    factors = {}
    for name, (base, spread) in spreads.items():
        noise = np.random.default_rng([zlib.crc32(name.encode()), seed]).standard_normal(out[name].shape)
        drawn = base * np.exp(spread * noise) if base else spread * noise
        out[name] = jnp.asarray(drawn.astype(out[name].dtype))
    for name, factor in factors.items():
        out[name] = (out[name] * factor).astype(out[name].dtype)
    return out
```

```python
from contextlib import ExitStack

import concourse.bass as bass
from concourse import mybir

ALU = mybir.AluOpType
ACT = mybir.ActivationFunctionType
F32 = mybir.dt.float32
F32R = mybir.dt.float32r

P = 128
G = 2
EPS = 1e-5
TINY = 1.1754944e-38


class Pair:

    def __init__(self, half, slot, pairs):
        self.half, self.slot, self.pairs = half, slot, pairs

    @property
    def number(self):
        return self.half * 2 + self.slot

    def back(self, n):
        moved = self.slot - n
        return Pair(self.half + moved // 2, moved % 2, self.pairs)

    def exists(self):
        return not isinstance(self.half, int) or 0 <= self.number < self.pairs


def wait(eng, sem, value):
    if not isinstance(value, int) or value > 0:
        eng.wait_ge(sem, value)


def build(nc, x, adj, w1, b1, gamma, beta, w2, b2, wq_w, wq_b, wk_w, wk_b, wv_w, wv_b, out):
    N, C, D = x.shape
    HID = w1.shape[0]
    DC, HC = D // P, HID // P
    PAIRS = N // G
    assert C == P and N % G == 0 and PAIRS % 2 == 0

    x_pairs = x.rearrange("(k g) c d -> k c g d", g=G)
    adj_pairs = adj.rearrange("(k g) c e -> k c g e", g=G)
    out_pairs = out.rearrange("(k g) c d -> k c g d", g=G)

    def over_pairs(eng, iteration):
        for k in range(4):
            iteration(Pair(k // 2, k % 2, PAIRS))
        with eng.Fori(2, PAIRS // 2 - 1) as half:
            for slot in (0, 1):
                iteration(Pair(half, slot, PAIRS))
        for k in range(PAIRS - 2, PAIRS + 2):
            iteration(Pair(k // 2, k % 2, PAIRS))

    with ExitStack() as ctx:
        def sb(name, shape, dt=F32):
            return ctx.enter_context(nc.sbuf_tensor(name, shape, dt))

        def sem(name):
            return ctx.enter_context(nc.semaphore(name))

        ident = sb("ident", [P, P])
        w1_nat = sb("w1_nat", [P, HC, D])
        w2_nat = sb("w2_nat", [P, DC, HID])
        wq_nat = sb("wq_nat", [P, DC, D])
        wk_nat = sb("wk_nat", [P, DC, D])
        wv_nat = sb("wv_nat", [P, DC, D])
        b1_rows = sb("b1_rows", [P, HID])
        b2_half = sb("b2_half", [P, D])
        bv_rows = sb("bv_rows", [P, D])
        gamma_col = sb("gamma_col", [P, HC])
        beta_col = sb("beta_col", [P, HC])
        bq_col = sb("bq_col", [P, DC])
        bk_col = sb("bk_col", [P, DC])
        w1T_hi = sb("w1T_hi", [P, DC, HID], F32R)
        w1T_lo = sb("w1T_lo", [P, DC, HID], F32R)
        w2T = sb("w2T", [P, HC, D])
        w2g = sb("w2g", [P, HC, D])
        w2g_hi = sb("w2g_hi", [P, HC, D], F32R)
        w2g_lo = sb("w2g_lo", [P, HC, D], F32R)
        wvT_hi = sb("wvT_hi", [P, DC, D + 2], F32R)
        wvT_lo = sb("wvT_lo", [P, DC, D + 2], F32R)
        mT_hi = sb("mT_hi", [P, DC, D], F32R)
        mT_lo = sb("mT_lo", [P, DC, D], F32R)
        bw2_half = sb("bw2_half", [P, D])
        small = sb("small", [P, 8])
        wkb, c2_col, bqbk = small[:, 0:DC], small[:, 2:2 + DC], small[:, 4:5]
        neg_half = sb("neg_half", [P, G])
        zero_row = sb("zero_row", [P, G])

        x_in = sb("x_in", [P, 2, G, D])
        adj_in = sb("adj_in", [P, 2, G, C])
        adjT = sb("adjT", [P, 2, G, C])
        hT = sb("hT", [P, G, C], F32R)
        count = sb("count", [P, G])
        be = sb("be", [P, G])
        be_hi = sb("be_hi", [P, G], F32R)
        be_lo = sb("be_lo", [P, G], F32R)
        hb_hi = sb("hb_hi", [P, G, C + 2], F32R)
        hb_lo = sb("hb_lo", [P, G, C + 2], F32R)
        s_mat = sb("s_mat", [P, 2, G, C + 2])
        dn_safe = sb("dn_safe", [P, G])
        dn_rec = sb("dn_rec", [P, G])
        dn = sb("dn", [P, 2, G])
        dn_deg = sb("dn_deg", [P, G])
        beta_term = sb("beta_term", [P, G, D])
        resid = sb("resid", [P, 2, G, D])
        sx_hi = sb("sx_hi", [P, G, DC, C], F32R)
        sx_lo = sb("sx_lo", [P, G, DC, C], F32R)
        h_pre = sb("h_pre", [P, G, HID])
        h_relu = sb("h_relu", [P, G, HID])
        h_norm = sb("h_norm", [P, G, HID])
        ln1_stats = sb("ln1_stats", [P, G, 6])
        ln1_mv = sb("ln1_mv", [P, G, 2])
        ln1_ve = sb("ln1_ve", [P, G])
        ln1_rstd = sb("ln1_rstd", [P, G])
        sh_hi = sb("sh_hi", [P, G, HC, C], F32R)
        sh_lo = sb("sh_lo", [P, G, HC, C], F32R)
        u = sb("u", [P, G, D])
        ln2_stats = sb("ln2_stats", [P, G, 6])
        ln2_mv = sb("ln2_mv", [P, G, 2])
        ln2_ve = sb("ln2_ve", [P, G])
        ln2_rstd = sb("ln2_rstd", [P, G])
        x1 = sb("x1", [P, G, D])
        x1_bv = sb("x1_bv", [P, G, D])
        x1T_hi = sb("x1T_hi", [P, DC, G, C], F32R)
        x1T_lo = sb("x1T_lo", [P, DC, G, C], F32R)
        zT_hi = sb("zT_hi", [P, DC, G, C], F32R)
        zT_lo = sb("zT_lo", [P, DC, G, C], F32R)
        val = sb("val", [P, G, D + 2])
        r_bias = sb("r_bias", [P, G])
        e_mat = sb("e_mat", [P, G, C])
        pT = sb("pT", [P, G, C])
        den_rec = sb("den_rec", [P, G])
        y_pre = sb("y_pre", [P, G, D])
        ln3_stats = sb("ln3_stats", [P, G, 6])
        ln3_mv = sb("ln3_mv", [P, G, 2])
        ln3_ve = sb("ln3_ve", [P, G])
        ln3_rstd = sb("ln3_rstd", [P, G])
        ln3_neg = sb("ln3_neg", [P, G])
        ln3_shift = sb("ln3_shift", [P, G])
        y = sb("y", [P, 2, G, D])

        bank = [ctx.enter_context(nc.psum_tensor(f"bank{n}", [P, 512], F32)) for n in range(8)]
        b_first = bank[0]
        b_out1 = bank[1:3]
        b_shT = bank[3:5]
        b_out2 = bank[5]
        b_attn = bank[6]
        b_val = bank[7]
        val_bank = [b_val, b_out2]
        att_bank = [b_val, b_attn]

        x_landed = [sem(f"x_landed{s}") for s in range(2)]
        adj_landed = [sem(f"adj_landed{s}") for s in range(2)]
        y_stored = [sem(f"y_stored{s}") for s in range(2)]
        w1_landed, w2_landed, wqk_landed, wv_landed = sem("w1_landed"), sem("w2_landed"), sem("wqk_landed"), sem("wv_landed")
        rows_landed, cols_landed = sem("rows_landed"), sem("cols_landed")
        ident_ready, ident_zeroed, consts_set = sem("ident_ready"), sem("ident_zeroed"), sem("consts_set")
        setup_pe, setup_act, setup_dve, b2_halved = sem("setup_pe"), sem("setup_act"), sem("setup_dve"), sem("b2_halved")
        adjT_done, s_done, sx_done = sem("adjT_done"), sem("s_done"), sem("sx_done")
        out1_g, shT_g, out2_g = sem("out1_g"), sem("shT_g"), sem("out2_g")
        x1T_done, zT_done, val_g, scores_done, att_done = sem("x1T_done"), sem("zT_done"), sem("val_g"), sem("scores_done"), sem("att_done")
        adjT_copied, s_copied, sx_hi_ready = sem("adjT_copied"), sem("s_copied"), sem("sx_hi_ready")
        relu_g, sh_hi_g, x1T_hi_ready, zT_hi_ready = sem("relu_g"), sem("sh_hi_g"), sem("x1T_hi_ready"), sem("zT_hi_ready")
        val_copied_g, exp_g, y_ready = sem("val_copied_g"), sem("exp_g"), sem("y_ready")
        hT_g, be_max, be_ready = sem("hT_g"), sem("be_max"), sem("be_ready")
        dn_clamped, dn_inverted, dn_ready = sem("dn_clamped"), sem("dn_inverted"), sem("dn_ready")
        sx_lo_ready, pre1_g, sh_lo_g = sem("sx_lo_ready"), sem("pre1_g"), sem("sh_lo_g")
        stats1_g, mv1_g, h_norm_g = sem("stats1_g"), sem("mv1_g"), sem("h_norm_g")
        u_g, stats2_g, mv2_g, x1_ready = sem("u_g"), sem("stats2_g"), sem("mv2_g"), sem("x1_ready")
        x1T_lo_ready, zT_lo_ready, r_ready = sem("x1T_lo_ready"), sem("zT_lo_ready"), sem("r_ready")
        den_ready, y_pre_g, stats3_g, mv3_g = sem("den_ready"), sem("y_pre_g"), sem("stats3_g"), sem("mv3_g")
        w_hi_ready, be_hi_ready, be_lo_ready, hb_ready = sem("w_hi_ready"), sem("be_hi_ready"), sem("be_lo_ready"), sem("hb_ready")
        dn_deg_ready, beta_scaled, beta_biased, resid_ready = sem("dn_deg_ready"), sem("beta_scaled"), sem("beta_biased"), sem("resid_ready")
        ve1_g, ve2_g, ve3_g = sem("ve1_g"), sem("ve2_g"), sem("ve3_g")
        rstd1, rstd2, rstd3 = sem("rstd1"), sem("rstd2"), sem("rstd3")
        neg3, shift3, x1_bv_ready, pT_ready = sem("neg3"), sem("shift3"), sem("x1_bv_ready"), sem("pT_ready")

        J_W1, J_SMALL, J_MT, J_WV, J_W2, J_BW2 = 1, 3, 4, 5, 6, 8
        SETUP_ACT, SETUP_DVE = 9, 14

        block = ctx.enter_context(nc.Block())

        @block.sync
        def _(sp):
            def load_adj(p):
                wait(sp, adjT_done, p.back(2).number + 1)
                sp.dma_start(adj_in[:, p.slot], adj_pairs[bass.ds(p.number, 1)].squeeze(0)).then_inc(adj_landed[p.slot], 16)

            def load_x(p):
                wait(sp, sx_done, p.back(2).number + 1)
                wait(sp, resid_ready, p.back(2).number + 1)
                sp.dma_start(x_in[:, p.slot], x_pairs[bass.ds(p.number, 1)].squeeze(0)).then_inc(x_landed[p.slot], 16)

            load_adj(Pair(0, 0, PAIRS))
            sp.dma_start(w1_nat[:, :, :], w1.rearrange("(c p) d -> p c d", p=P)).then_inc(w1_landed, 16)
            load_x(Pair(0, 0, PAIRS))
            load_adj(Pair(0, 1, PAIRS))
            sp.dma_start(w2_nat[:, :, :], w2.rearrange("(c p) d -> p c d", p=P)).then_inc(w2_landed, 16)

            def iteration(p):
                if p.back(-1).exists():
                    load_x(p.back(-1))
                if p.back(-2).exists():
                    load_adj(p.back(-2))
                q = p.back(2)
                if q.exists():
                    wait(sp, y_ready, G * q.number + G)
                    sp.dma_start(out_pairs[bass.ds(q.number, 1)].squeeze(0), y[:, q.slot]).then_inc(y_stored[q.slot], 16)

            over_pairs(sp, iteration)
            for s in range(2):
                sp.wait_ge(y_stored[s], 16 * (PAIRS // 2))

        @block.tensor
        def _(pe):
            def three_passes(psum, hi, lo, r_hi, r_lo, start, stop):
                pe.matmul(psum, hi, r_hi, start=start, stop=False)
                pe.matmul(psum, hi, r_lo, start=False, stop=False)
                return pe.matmul(psum, lo, r_hi, start=False, stop=stop)

            def transpose_adj(p):
                if not p.exists():
                    return
                wait(pe, adj_landed[p.slot], p.half * 16 + 16)
                wait(pe, sx_lo_ready, p.back(1).number + 1)
                for g in range(G):
                    last = pe.transpose(b_first[:, g * C:(g + 1) * C], adj_in[:, p.slot, g, :], ident[:, :])
                last.then_inc(adjT_done, 1)

            pe.wait_ge(ident_ready, 1)
            pe.wait_ge(w1_landed, 16)
            for dc in range(DC):
                for hc in range(HC):
                    last = pe.transpose(b_out1[dc][:, hc * P:(hc + 1) * P], w1_nat[:, hc, dc * P:(dc + 1) * P], ident[:, :])
                last.then_inc(setup_pe, 1)
            pe.wait_ge(wqk_landed, 32)
            pe.wait_ge(cols_landed, 64)
            for col, w, b in ((0, wk_nat, bq_col), (2, wq_nat, bk_col)):
                for dc in range(DC):
                    for oc in range(DC):
                        pe.matmul(b_attn[:, col + dc:col + dc + 1], w[:, oc, dc * P:(dc + 1) * P], b[:, oc:oc + 1],
                                  start=(oc == 0), stop=(oc == DC - 1))
            for oc in range(DC):
                last = pe.matmul(b_attn[:, 4:5], bq_col[:, oc:oc + 1].to_broadcast([P, P]), bk_col[:, oc:oc + 1],
                                 start=(oc == 0), stop=(oc == DC - 1))
            last.then_inc(setup_pe, 1)
            for kc in range(DC):
                for oc in range(DC):
                    last = pe.matmul(b_val[:, kc * D:(kc + 1) * D], wk_nat[:, oc, kc * P:(kc + 1) * P], wq_nat[:, oc, :],
                                     start=(oc == 0), stop=(oc == DC - 1))
            last.then_inc(setup_pe, 1)
            pe.wait_ge(wv_landed, 16)
            for dc in range(DC):
                for oc in range(DC):
                    last = pe.transpose(b_out2[:, dc * D + oc * P:dc * D + (oc + 1) * P],
                                        wv_nat[:, oc, dc * P:(dc + 1) * P], ident[:, :])
            last.then_inc(setup_pe, 1)
            pe.wait_ge(w2_landed, 16)
            for hc in range(HC):
                for oc in range(DC):
                    last = pe.transpose(b_shT[hc // 2][:, (hc % 2) * D + oc * P:(hc % 2) * D + (oc + 1) * P],
                                        w2_nat[:, oc, hc * P:(hc + 1) * P], ident[:, :])
                if hc % 2:
                    last.then_inc(setup_pe, 1)
            pe.wait_ge(setup_act, 8)
            for hc in range(HC):
                last = pe.matmul(b_first[:, 0:D], beta_col[:, hc:hc + 1].to_broadcast([P, P]), w2T[:, hc, :],
                                 start=(hc == 0), stop=(hc == HC - 1))
            last.then_inc(setup_pe, 1)
            pe.wait_ge(setup_act, SETUP_ACT)
            pe.wait_ge(setup_dve, SETUP_DVE)
            transpose_adj(Pair(0, 0, PAIRS))

            def iteration(p):
                a, b, c = p, p.back(1), p.back(2)
                last_a = a.exists()
                if b.exists():
                    for g in range(G):
                        wait(pe, h_norm_g, G * b.number + g + 1)
                        wait(pe, sh_lo_g, G * b.back(1).number + g + 1)
                        for hc in range(HC):
                            last = pe.matmul(b_shT[g][:, hc * C:(hc + 1) * C], h_norm[:, g, hc * P:(hc + 1) * P],
                                             s_mat[:, b.slot, g, 0:C], start=True, stop=True)
                        last.then_inc(shT_g, 1)
                if c.exists():
                    wait(pe, pT_ready, c.number + 1)
                    wait(pe, val_copied_g, G * c.number + G)
                    wait(pe, exp_g, G * c.number + G)
                    for g in range(G):
                        last = pe.matmul(att_bank[g][:, 0:D + 2], pT[:, g, :], val[:, g, :], start=True, stop=True)
                    last.then_inc(att_done, 1)
                if last_a:
                    wait(pe, hb_ready, a.number + 1)
                    wait(pe, hT_g, G * a.number + G)
                    wait(pe, adjT_copied, a.number + 1)
                    for g in range(G):
                        dst = b_first[:, g * (C + 2):(g + 1) * (C + 2)]
                        pe.matmul(dst, hT[:, g, :], hb_hi[:, g, :], start=True, stop=False)
                        last = pe.matmul(dst, hT[:, g, :], hb_lo[:, g, :], start=False, stop=True)
                    last.then_inc(s_done, 1)

                def out2(g):
                    wait(pe, sh_hi_g, G * b.number + g + 1)
                    wait(pe, sh_lo_g, G * b.number + g + 1)
                    if g == 0:
                        wait(pe, val_copied_g, G * b.back(1).number + G)
                    for hc in range(HC):
                        last = three_passes(b_out2[:, g * D:(g + 1) * D], sh_hi[:, g, hc, :], sh_lo[:, g, hc, :],
                                            w2g_hi[:, hc, :], w2g_lo[:, hc, :], hc == 0, hc == HC - 1)
                    last.then_inc(out2_g, 1)

                if b.exists():
                    out2(0)
                if last_a:
                    wait(pe, s_copied, a.number + 1)
                    wait(pe, x_landed[a.slot], a.half * 16 + 16)
                    for g in range(G):
                        for dc in range(DC):
                            last = pe.matmul(b_first[:, (g * DC + dc) * C:(g * DC + dc + 1) * C],
                                             x_in[:, a.slot, g, dc * P:(dc + 1) * P], s_mat[:, a.slot, g, 0:C],
                                             start=True, stop=True)
                    last.then_inc(sx_done, 1)
                if b.exists():
                    out2(1)
                if last_a:
                    wait(pe, sx_hi_ready, a.number + 1)
                    wait(pe, sx_lo_ready, a.number + 1)
                    for g in range(G):
                        wait(pe, pre1_g, G * a.back(1).number + g + 1)
                        for dc in range(DC):
                            last = three_passes(b_out1[g][:, :], sx_hi[:, g, dc, :], sx_lo[:, g, dc, :],
                                                w1T_hi[:, dc, :], w1T_lo[:, dc, :], dc == 0, dc == DC - 1)
                        last.then_inc(out1_g, 1)
                if b.exists():
                    wait(pe, x1_ready, b.number + 1)
                    wait(pe, y_pre_g, G * b.back(1).number + G)
                    for dc in range(DC):
                        for g in range(G):
                            last = pe.transpose(b_attn[:, (dc * G + g) * C:(dc * G + g + 1) * C],
                                                x1[:, g, dc * P:(dc + 1) * P], ident[:, :])
                    last.then_inc(x1T_done, 1)
                    wait(pe, x1T_hi_ready, b.number + 1)
                    wait(pe, x1T_lo_ready, b.number + 1)
                    for dc in range(DC):
                        for kc in range(DC):
                            last = three_passes(b_attn[:, dc * G * C:(dc + 1) * G * C],
                                                mT_hi[:, kc, dc * P:(dc + 1) * P], mT_lo[:, kc, dc * P:(dc + 1) * P],
                                                x1T_hi[:, kc, :, :], x1T_lo[:, kc, :, :], kc == 0, kc == DC - 1)
                    last.then_inc(zT_done, 1)
                    wait(pe, u_g, G * b.number + G)
                    for g in range(G):
                        for dc in range(DC):
                            last = three_passes(val_bank[g][:, 0:D + 2], x1T_hi[:, dc, g, :], x1T_lo[:, dc, g, :],
                                                wvT_hi[:, dc, :], wvT_lo[:, dc, :], dc == 0, dc == DC - 1)
                        last.then_inc(val_g, 1)
                    wait(pe, zT_hi_ready, b.number + 1)
                    wait(pe, zT_lo_ready, b.number + 1)
                    for g in range(G):
                        for dc in range(DC):
                            last = three_passes(b_attn[:, g * C:(g + 1) * C], zT_hi[:, dc, g, :], zT_lo[:, dc, g, :],
                                                x1T_hi[:, dc, g, :], x1T_lo[:, dc, g, :], dc == 0, dc == DC - 1)
                    last.then_inc(scores_done, 1)
                transpose_adj(p.back(-1))

            over_pairs(pe, iteration)

        @block.scalar
        def _(act):
            act.dma_start(wq_nat[:, :, :], wq_w.rearrange("(c p) d -> p c d", p=P)).then_inc(wqk_landed, 16)
            act.dma_start(wk_nat[:, :, :], wk_w.rearrange("(c p) d -> p c d", p=P)).then_inc(wqk_landed, 16)
            act.dma_start(wv_nat[:, :, :], wv_w.rearrange("(c p) d -> p c d", p=P)).then_inc(wv_landed, 16)
            act.dma_start(b1_rows[:, :], b1.partition_broadcast(P)).then_inc(rows_landed, 16)
            act.dma_start(b2_half[:, :], b2.partition_broadcast(P)).then_inc(rows_landed, 16)
            act.dma_start(bv_rows[:, :], wv_b.partition_broadcast(P)).then_inc(rows_landed, 16)

            for dc in range(DC):
                act.wait_ge(setup_pe, J_W1 + dc)
                act.activation(w1T_hi[:, dc, :], b_out1[dc][:, :], ACT.Copy).then_inc(setup_act, 1)
            act.wait_ge(setup_pe, J_SMALL)
            act.activation(small[:, 0:5], b_attn[:, 0:5], ACT.Copy).then_inc(setup_act, 1)
            act.wait_ge(setup_pe, J_MT)
            act.activation(mT_hi[:, :, :], b_val[:, :].rearrange("p (c d) -> p c d", c=DC), ACT.Copy).then_inc(setup_act, 1)
            act.wait_ge(setup_pe, J_WV)
            act.activation(wvT_hi[:, :, 0:D], b_out2[:, :].rearrange("p (c d) -> p c d", c=DC), ACT.Copy).then_inc(setup_act, 1)
            act.wait_ge(setup_act, 3)
            act.activation(wvT_hi[:, :, D:D + 1], wkb.unsqueeze(2), ACT.Copy).then_inc(setup_act, 1)
            for j in range(2):
                act.wait_ge(setup_pe, J_W2 + j)
                act.activation(w2T[:, 2 * j:2 * j + 2, :], b_shT[j][:, :].rearrange("p (c d) -> p c d", c=2),
                               ACT.Copy).then_inc(setup_act, 1)
            act.wait_ge(setup_dve, 9)
            act.activation(w2g_hi[:, :, :], w2g[:, :, :], ACT.Copy).then_inc(setup_act, 1)

            def copy_adjT(p):
                if not p.exists():
                    return
                wait(act, adjT_done, p.number + 1)
                wait(act, pT_ready, p.back(2).number + 1)
                wait(act, hT_g, G * p.back(2).number + G)
                act.activation(adjT[:, p.slot], b_first[:, 0:G * C].rearrange("p (g c) -> p g c", g=G),
                               ACT.Copy).then_inc(adjT_copied, 1)

            copy_adjT(Pair(0, 0, PAIRS))

            def iteration(p):
                a, b, c = p, p.back(1), p.back(2)
                if b.exists():
                    for g in range(G):
                        wait(act, shT_g, G * b.number + g + 1)
                        wait(act, out2_g, G * b.back(1).number + g + 1)
                        act.activation(sh_hi[:, g], b_shT[g][:, :].rearrange("p (c n) -> p c n", c=HC),
                                       ACT.Copy).then_inc(sh_hi_g, 1)
                if a.exists():
                    wait(act, s_done, a.number + 1)
                    wait(act, shT_g, G * a.back(2).number + G)
                    wait(act, resid_ready, a.back(2).number + 1)
                    act.activation(s_mat[:, a.slot], b_first[:, 0:G * (C + 2)].rearrange("p (g c) -> p g c", g=G),
                                   ACT.Copy).then_inc(s_copied, 1)
                    wait(act, sx_done, a.number + 1)
                    wait(act, out1_g, G * a.back(1).number + G)
                    act.activation(sx_hi[:, :, :, :], b_first[:, :].rearrange("p (g c n) -> p g c n", g=G, c=DC),
                                   ACT.Copy).then_inc(sx_hi_ready, 1)
                    for g in range(G):
                        wait(act, pre1_g, G * a.number + g + 1)
                        wait(act, h_norm_g, G * a.back(1).number + g + 1)
                        act.activation(h_relu[:, g, :], h_pre[:, g, :], ACT.Relu).then_inc(relu_g, 1)
                if c.exists():
                    wait(act, shift3, c.number + 1)
                    wait(act, y_stored[c.slot], c.half * 16)
                    for g in range(G):
                        act.activation(y[:, c.slot, g, :], y_pre[:, g, :], ACT.Identity, scale=ln3_rstd[:, g:g + 1],
                                       bias=ln3_shift[:, g:g + 1]).then_inc(y_ready, 1)
                if b.exists():
                    wait(act, x1T_done, b.number + 1)
                    wait(act, scores_done, b.back(1).number + 1)
                    act.activation(x1T_hi[:, :, :, :], b_attn[:, :].rearrange("p (c g n) -> p c g n", c=DC, g=G),
                                   ACT.Copy).then_inc(x1T_hi_ready, 1)
                    wait(act, zT_done, b.number + 1)
                    for dc in range(DC):
                        last = act.activation(zT_hi[:, dc].rearrange("p g n -> p (g n)"), b_attn[:, dc * G * C:(dc + 1) * G * C],
                                              ACT.Identity, bias=c2_col[:, dc:dc + 1])
                    last.then_inc(zT_hi_ready, 1)
                    for g in range(G):
                        wait(act, val_g, G * b.number + g + 1)
                        wait(act, att_done, b.back(1).number + 1)
                        act.activation(val[:, g, 0:D + 1], val_bank[g][:, 0:D + 1], ACT.Copy).then_inc(val_copied_g, 1)
                    wait(act, scores_done, b.number + 1)
                    wait(act, r_ready, b.number + 1)
                    for g in range(G):
                        wait(act, pT_ready, b.back(1).number + 1)
                        act.activation(e_mat[:, g, :], b_attn[:, g * C:(g + 1) * C], ACT.Exp,
                                       bias=r_bias[:, g:g + 1]).then_inc(exp_g, 1)
                copy_adjT(p.back(-1))

            over_pairs(act, iteration)

        @block.vector
        def _(dve):
            dve.wait_ge(rows_landed, 48)
            dve.tensor_scalar(b2_half[:, :], b2_half[:, :], 0.5, None, ALU.mult).then_inc(b2_halved, 1)
            for dc in range(DC):
                dve.wait_ge(setup_act, 1 + dc)
                dve.tensor_tensor(w1T_lo[:, dc, :], b_out1[dc][:, :], w1T_hi[:, dc, :].bitcast(F32),
                                  ALU.subtract).then_inc(setup_dve, 1)
            dve.wait_ge(setup_act, 4)
            dve.tensor_tensor(mT_lo[:, :, :], b_val[:, :].rearrange("p (c d) -> p c d", c=DC), mT_hi[:, :, :].bitcast(F32),
                              ALU.subtract).then_inc(setup_dve, 1)
            dve.wait_ge(setup_act, 5)
            dve.tensor_tensor(wvT_lo[:, :, 0:D], b_out2[:, :].rearrange("p (c d) -> p c d", c=DC),
                              wvT_hi[:, :, 0:D].bitcast(F32), ALU.subtract).then_inc(setup_dve, 1)
            dve.wait_ge(setup_act, 6)
            dve.tensor_tensor(wvT_lo[:, :, D:D + 1], wkb.unsqueeze(2), wvT_hi[:, :, D:D + 1].bitcast(F32),
                              ALU.subtract).then_inc(setup_dve, 1)
            dve.wait_ge(cols_landed, 64)
            for hc in range(HC):
                dve.wait_ge(setup_act, 7 + hc // 2)
                dve.tensor_scalar(w2g[:, hc, :], b_shT[hc // 2][:, (hc % 2) * D:(hc % 2 + 1) * D],
                                  gamma_col[:, hc:hc + 1], 0.5, ALU.mult, ALU.mult).then_inc(setup_dve, 1)
            dve.wait_ge(setup_act, 9)
            dve.tensor_tensor(w2g_lo[:, :, :], w2g[:, :, :], w2g_hi[:, :, :].bitcast(F32), ALU.subtract).then_inc(setup_dve, 1)
            dve.wait_ge(setup_pe, J_BW2)
            dve.tensor_scalar(bw2_half[:, :], b_first[:, 0:D], 0.5, None, ALU.mult).then_inc(setup_dve, 1)
            dve.wait_ge(consts_set, 3)
            for t in (wvT_hi, wvT_lo):
                dve.tensor_copy(t[:, :, D + 1:D + 2], zero_row[:, :].unsqueeze(2)).then_inc(setup_dve, 1)
            dve.tensor_copy(hb_hi[:, :, C + 1:C + 2], val[:, :, D + 1:D + 2]).then_inc(setup_dve, 1)
            dve.tensor_copy(hb_lo[:, :, C + 1:C + 2], zero_row[:, :].unsqueeze(2)).then_inc(setup_dve, 1)

            def incidence(p):
                if not p.exists():
                    return
                wait(dve, adjT_copied, p.number + 1)
                wait(dve, s_done, p.back(1).number + 1)
                wait(dve, hb_ready, p.back(1).number + 1)
                for g in range(G):
                    dve.tensor_scalar(hT[:, g, :], adjT[:, p.slot, g, :], 0.0, None, ALU.not_equal, ALU.add,
                                      accum_out=count[:, g:g + 1]).then_inc(hT_g, 1)
                wait(dve, hT_g, G * p.number + G)
                dve.tensor_scalar(be[:, :], count[:, :], 1.0, None, ALU.max).then_inc(be_max, 1)
                wait(dve, be_max, p.number + 1)
                dve.reciprocal(be[:, :], be[:, :]).then_inc(be_ready, 1)

            incidence(Pair(0, 0, PAIRS))

            def moments(p, src, src_g, stats, stats_g, mv, mv_g, eps, ve, ve_g, taken):
                wait(dve, src_g, G * p.number + 1)
                dve.bn_stats(stats[:, 0, :], src[:, 0, :]).then_inc(stats_g, 1)
                wait(dve, taken, p.number)
                wait(dve, stats_g, G * p.number + 1)
                wait(dve, src_g, G * p.number + 2)
                dve.bn_stats(stats[:, 1, :], src[:, 1, :]).then_inc(stats_g, 1)
                dve.bn_aggr(mv[:, 0, :], stats[:, 0, :]).then_inc(mv_g, 1)
                wait(dve, stats_g, G * p.number + 2)
                wait(dve, mv_g, G * p.number + 1)
                dve.tensor_scalar(ve[:, 0:1], mv[:, 0, 1:2], eps, None, ALU.add).then_inc(ve_g, 1)
                dve.bn_aggr(mv[:, 1, :], stats[:, 1, :]).then_inc(mv_g, 1)
                wait(dve, mv_g, G * p.number + 2)
                dve.tensor_scalar(ve[:, 1:2], mv[:, 1, 1:2], eps, None, ALU.add).then_inc(ve_g, 1)

            def iteration(p):
                a, b, c = p, p.back(1), p.back(2)
                if b.exists():
                    for g in range(G):
                        wait(dve, sh_hi_g, G * b.number + g + 1)
                        wait(dve, out2_g, G * b.back(1).number + g + 1)
                        dve.tensor_tensor(sh_lo[:, g], b_shT[g][:, :].rearrange("p (c n) -> p c n", c=HC),
                                          sh_hi[:, g].bitcast(F32), ALU.subtract).then_inc(sh_lo_g, 1)
                if a.exists():
                    wait(dve, s_copied, a.number + 1)
                    sums = s_mat[:, a.slot, :, C]
                    dve.tensor_scalar(dn_safe[:, :], sums, TINY, None, ALU.max).then_inc(dn_clamped, 1)
                    wait(dve, dn_clamped, a.number + 1)
                    dve.reciprocal(dn_rec[:, :], dn_safe[:, :]).then_inc(dn_inverted, 1)
                    wait(dve, dn_inverted, a.number + 1)
                    wait(dve, resid_ready, a.back(2).number + 1)
                    dve.scalar_tensor_tensor(dn[:, a.slot, :], sums, 0.0, dn_rec[:, :], ALU.is_gt,
                                             ALU.mult).then_inc(dn_ready, 1)
                if c.exists():
                    wait(dve, att_done, c.number + 1)
                    for g in range(G):
                        dve.reciprocal(den_rec[:, g:g + 1], att_bank[g][:, D + 1:D + 2]).then_inc(den_ready, 1)
                    wait(dve, x1_bv_ready, c.number + 1)
                    wait(dve, y_ready, G * c.back(1).number + G)
                    for g in range(G):
                        wait(dve, den_ready, G * c.number + g + 1)
                        dve.scalar_tensor_tensor(y_pre[:, g, :], att_bank[g][:, 0:D], den_rec[:, g:g + 1], x1_bv[:, g, :],
                                                 ALU.mult, ALU.add).then_inc(y_pre_g, 1)
                    moments(c, y_pre, y_pre_g, ln3_stats, stats3_g, ln3_mv, mv3_g, EPS, ln3_ve, ve3_g, shift3)

                def second(g):
                    wait(dve, out2_g, G * b.number + g + 1)
                    wait(dve, resid_ready, b.number + 1)
                    dve.scalar_tensor_tensor(u[:, g, :], b_out2[:, g * D:(g + 1) * D], dn[:, b.slot, g:g + 1],
                                             resid[:, b.slot, g, :], ALU.mult, ALU.add).then_inc(u_g, 1)

                if a.exists():
                    wait(dve, sx_hi_ready, a.number + 1)
                    wait(dve, out1_g, G * a.back(1).number + G)
                    dve.tensor_tensor(sx_lo[:, :, :, :], b_first[:, :].rearrange("p (g c n) -> p g c n", g=G, c=DC),
                                      sx_hi[:, :, :, :].bitcast(F32), ALU.subtract).then_inc(sx_lo_ready, 1)
                if b.exists():
                    wait(dve, out2_g, G * b.number + G)
                    for g in range(G):
                        second(g)
                    moments(b, u, u_g, ln2_stats, stats2_g, ln2_mv, mv2_g, EPS / 4, ln2_ve, ve2_g, rstd2)

                def first(g):
                    wait(dve, dn_ready, a.number + 1)
                    wait(dve, out1_g, G * a.number + g + 1)
                    wait(dve, relu_g, G * a.back(1).number + g + 1)
                    dve.scalar_tensor_tensor(h_pre[:, g, :], b_out1[g][:, :], dn[:, a.slot, g:g + 1], b1_rows[:, :],
                                             ALU.mult, ALU.add).then_inc(pre1_g, 1)

                if a.exists():
                    first(0)
                if b.exists():
                    wait(dve, rstd2, b.number + 1)
                    for g in range(G):
                        last = dve.tensor_scalar(x1[:, g, :], u[:, g, :], ln2_mv[:, g, 0:1], ln2_rstd[:, g:g + 1],
                                                 ALU.subtract, ALU.mult)
                    last.then_inc(x1_ready, 1)
                if a.exists():
                    first(1)

                if b.exists():
                    wait(dve, x1T_hi_ready, b.number + 1)
                    wait(dve, scores_done, b.back(1).number + 1)
                    dve.tensor_tensor(x1T_lo[:, :, :, :], b_attn[:, :].rearrange("p (c g n) -> p c g n", c=DC, g=G),
                                      x1T_hi[:, :, :, :].bitcast(F32), ALU.subtract).then_inc(x1T_lo_ready, 1)
                if a.exists():
                    moments(a, h_relu, relu_g, ln1_stats, stats1_g, ln1_mv, mv1_g, EPS, ln1_ve, ve1_g, rstd1)
                if b.exists():
                    wait(dve, zT_hi_ready, b.number + 1)
                    for dc in range(DC):
                        last = dve.scalar_tensor_tensor(
                            zT_lo[:, dc].rearrange("p g n -> p (g n)"), b_attn[:, dc * G * C:(dc + 1) * G * C],
                            c2_col[:, dc:dc + 1], zT_hi[:, dc].rearrange("p g n -> p (g n)").bitcast(F32),
                            ALU.add, ALU.subtract)
                    last.then_inc(zT_lo_ready, 1)
                if a.exists():
                    wait(dve, rstd1, a.number + 1)
                    for g in range(G):
                        wait(dve, shT_g, G * a.back(1).number + g + 1)
                        dve.tensor_scalar(h_norm[:, g, :], h_relu[:, g, :], ln1_mv[:, g, 0:1], ln1_rstd[:, g:g + 1],
                                          ALU.subtract, ALU.mult).then_inc(h_norm_g, 1)
                if b.exists():
                    wait(dve, val_copied_g, G * b.number + G)
                    wait(dve, exp_g, G * b.back(1).number + G)
                    dve.tensor_scalar(r_bias[:, :], val[:, :, D], bqbk, None, ALU.add).then_inc(r_ready, 1)
                incidence(p.back(-1))

            over_pairs(dve, iteration)

        @block.gpsimd
        def _(pool):
            pool.memset(ident[:, :], 0.0).then_inc(ident_zeroed, 1)
            for t, v in ((gamma_col, gamma), (beta_col, beta)):
                pool.dma_start(t[:, :], v.rearrange("(c p) -> p c", p=P), allow_slow_non_contiguous=True).then_inc(cols_landed, 16)
            for t, v in ((bq_col, wq_b), (bk_col, wk_b)):
                pool.dma_start(t[:, :], v.rearrange("(c p) -> p c", p=P), allow_slow_non_contiguous=True).then_inc(cols_landed, 16)
            pool.wait_ge(ident_zeroed, 1)
            pool.affine_select(out=ident[:, :], in_=ident[:, :], compare_op=ALU.not_equal, fill=1.0, base=0,
                               pattern=[[-1, P]], channel_multiplier=1).then_inc(ident_ready, 1)
            pool.memset(neg_half[:, :], -0.5).then_inc(consts_set, 1)
            pool.memset(zero_row[:, :], 0.0).then_inc(consts_set, 1)
            pool.memset(val[:, :, D + 1:D + 2], 1.0).then_inc(consts_set, 1)

            def edge_weights(p):
                if not p.exists():
                    return
                wait(pool, adjT_copied, p.number + 1)
                wait(pool, s_done, p.back(1).number + 1)
                w_row = adjT[:, p.slot, :, 0:1]
                pool.tensor_tensor(hb_hi[:, :, C:C + 1], w_row, zero_row[:, :].unsqueeze(2), ALU.add).then_inc(w_hi_ready, 1)
                wait(pool, be_ready, p.number + 1)
                pool.tensor_tensor(be_hi[:, :], be[:, :], zero_row[:, :], ALU.add).then_inc(be_hi_ready, 1)
                wait(pool, w_hi_ready, p.number + 1)
                pool.tensor_tensor(hb_lo[:, :, C:C + 1], w_row, hb_hi[:, :, C:C + 1].bitcast(F32), ALU.subtract)
                wait(pool, be_hi_ready, p.number + 1)
                pool.tensor_tensor(be_lo[:, :], be[:, :], be_hi[:, :].bitcast(F32), ALU.subtract).then_inc(be_lo_ready, 1)
                wait(pool, hT_g, G * p.number + G)
                pool.tensor_tensor(hb_hi[:, :, 0:C], hT[:, :, :].bitcast(F32),
                                   be_hi[:, :].bitcast(F32).unsqueeze(2).to_broadcast([P, G, C]), ALU.mult)
                wait(pool, be_lo_ready, p.number + 1)
                pool.tensor_tensor(hb_lo[:, :, 0:C], hT[:, :, :].bitcast(F32),
                                   be_lo[:, :].bitcast(F32).unsqueeze(2).to_broadcast([P, G, C]),
                                   ALU.mult).then_inc(hb_ready, 1)

            def rsqrt(p, ve, ve_g, rstd, rstd_done):
                wait(pool, ve_g, G * p.number + G)
                pool.tensor_tensor(rstd[:, :], ve[:, :], neg_half[:, :], ALU.pow).then_inc(rstd_done, 1)

            pool.wait_ge(consts_set, 3)
            pool.wait_ge(setup_dve, SETUP_DVE)
            pool.wait_ge(b2_halved, 1)
            edge_weights(Pair(0, 0, PAIRS))

            def iteration(p):
                a, b, c = p, p.back(1), p.back(2)
                if c.exists():
                    wait(pool, y_ready, G * c.back(1).number + G)
                    rsqrt(c, ln3_ve, ve3_g, ln3_rstd, rstd3)
                    pool.tensor_tensor(ln3_neg[:, :], zero_row[:, :], ln3_mv[:, :, 0], ALU.subtract).then_inc(neg3, 1)
                    wait(pool, neg3, c.number + 1)
                    wait(pool, rstd3, c.number + 1)
                    pool.tensor_tensor(ln3_shift[:, :], ln3_neg[:, :], ln3_rstd[:, :], ALU.mult).then_inc(shift3, 1)
                if a.exists():
                    wait(pool, dn_ready, a.number + 1)
                    pool.tensor_tensor(dn_deg[:, :], dn[:, a.slot, :], s_mat[:, a.slot, :, C + 1], ALU.mult).then_inc(dn_deg_ready, 1)
                    wait(pool, dn_deg_ready, a.number + 1)
                    pool.tensor_tensor(beta_term[:, :, :], bw2_half[:, :].unsqueeze(1).to_broadcast([P, G, D]),
                                       dn_deg[:, :].unsqueeze(2).to_broadcast([P, G, D]), ALU.mult).then_inc(beta_scaled, 1)
                    wait(pool, beta_scaled, a.number + 1)
                    pool.tensor_tensor(beta_term[:, :, :], beta_term[:, :, :],
                                       b2_half[:, :].unsqueeze(1).to_broadcast([P, G, D]), ALU.add).then_inc(beta_biased, 1)
                    wait(pool, beta_biased, a.number + 1)
                    wait(pool, x_landed[a.slot], a.half * 16 + 16)
                    wait(pool, u_g, G * a.back(2).number + G)
                    pool.tensor_tensor(resid[:, a.slot], x_in[:, a.slot], beta_term[:, :, :], ALU.add).then_inc(resid_ready, 1)
                if b.exists():
                    wait(pool, x1_ready, b.back(1).number + 1)
                    rsqrt(b, ln2_ve, ve2_g, ln2_rstd, rstd2)
                    wait(pool, x1_ready, b.number + 1)
                    wait(pool, y_pre_g, G * b.back(1).number + G)
                    pool.tensor_tensor(x1_bv[:, :, :], x1[:, :, :], bv_rows[:, :].unsqueeze(1).to_broadcast([P, G, D]),
                                       ALU.add).then_inc(x1_bv_ready, 1)
                if a.exists():
                    wait(pool, h_norm_g, G * a.back(1).number + G)
                    rsqrt(a, ln1_ve, ve1_g, ln1_rstd, rstd1)
                if b.exists():
                    wait(pool, exp_g, G * b.number + G)
                    wait(pool, att_done, b.back(1).number + 1)
                    pool.tensor_tensor(pT[:, :, :], adjT[:, b.slot], e_mat[:, :, :], ALU.mult).then_inc(pT_ready, 1)
                edge_weights(p.back(-1))

            over_pairs(pool, iteration)


_INS = ['x', 'adj', 'L0_gnn_W1', 'L0_gnn_b1', 'L0_gnn_gamma', 'L0_gnn_beta', 'L0_gnn_W2', 'L0_gnn_b2',
        'L1_gnn_Wq_w', 'L1_gnn_Wq_b', 'L1_gnn_Wk_w', 'L1_gnn_Wk_b', 'L1_gnn_Wv_w', 'L1_gnn_Wv_b']


def kernel(**inputs):
    import numpy as _np
    import concourse.bacc as _bacc
    from concourse import mybir as _mybir
    from concourse.bass_utils import run_bass_kernel_spmd as _run

    nc = _bacc.Bacc("TRN2", target_bir_lowering=False, num_devices=1)
    arrays, args = {}, []
    for name in _INS:
        a = _np.ascontiguousarray(inputs[name])
        arrays[f"in_{name}_dram"] = a
        args.append(nc.dram_tensor(f"in_{name}_dram", a.shape, _mybir.dt.from_np(a.dtype), kind="ExternalInput").ap())
    shape = arrays["in_x_dram"].shape
    args.append(nc.dram_tensor("out_dram", shape, _mybir.dt.float32, kind="ExternalOutput").ap())
    build(nc, *args)
    r = _run(nc, [arrays], core_ids=[0])
    return r.results[0]["out_dram"]
```

```python
from contextlib import ExitStack

import concourse.bass as bass
from concourse import mybir

ALU = mybir.AluOpType
ACT = mybir.ActivationFunctionType
F32 = mybir.dt.float32
F32R = mybir.dt.float32r

P = 128
G = 2
RING = 3
EPS = 1e-5
TINY = 1.1754944e-38


class Pair:

    def __init__(self, lap, slot, pairs):
        self.lap, self.slot, self.pairs = lap, slot, pairs

    @property
    def number(self):
        return self.lap * RING + self.slot

    def back(self, n):
        moved = self.slot - n
        return Pair(self.lap + moved // RING, moved % RING, self.pairs)

    def exists(self):
        return not isinstance(self.lap, int) or 0 <= self.number < self.pairs


def wait(eng, sem, value):
    if not isinstance(value, int) or value > 0:
        eng.wait_ge(sem, value)


def build(nc, x, adj, w1, b1, gamma, beta, w2, b2, wq_w, wq_b, wk_w, wk_b, wv_w, wv_b, out):
    N, C, D = x.shape
    HID = w1.shape[0]
    DC, HC = D // P, HID // P
    PAIRS = N // G
    assert C == P and N % G == 0

    x_pairs = x.rearrange("(k g) c d -> k c g d", g=G)
    adj_pairs = adj.rearrange("(k g) c e -> k c g e", g=G)
    out_pairs = out.rearrange("(k g) c d -> k c g d", g=G)

    LAG = 4
    LOOP_FROM = 2
    LOOP_TO = (PAIRS - 1) // RING

    def pair(k):
        return Pair(k // RING, k % RING, PAIRS)

    def over_pairs(eng, iteration):
        for k in range(LOOP_FROM * RING):
            iteration(pair(k))
        with eng.Fori(LOOP_FROM, LOOP_TO) as lap:
            for slot in range(RING):
                iteration(Pair(lap, slot, PAIRS))
        for k in range(LOOP_TO * RING, PAIRS + LAG):
            iteration(pair(k))

    with ExitStack() as ctx:
        def sb(name, shape, dt=F32):
            return ctx.enter_context(nc.sbuf_tensor(name, shape, dt))

        def sem(name):
            return ctx.enter_context(nc.semaphore(name))

        ident = sb("ident", [P, P])
        w1_nat = sb("w1_nat", [P, HC, D])
        w2_nat = sb("w2_nat", [P, DC, HID])
        wq_nat = sb("wq_nat", [P, DC, D])
        wk_nat = sb("wk_nat", [P, DC, D])
        wv_nat = sb("wv_nat", [P, DC, D])
        b1_rows = sb("b1_rows", [P, HID])
        b2_half = sb("b2_half", [P, D])
        bv_rows = sb("bv_rows", [P, D])
        gamma_col = sb("gamma_col", [P, HC])
        beta_col = sb("beta_col", [P, HC])
        bq_col = sb("bq_col", [P, DC])
        bk_col = sb("bk_col", [P, DC])
        w1T_hi = sb("w1T_hi", [P, DC, HID], F32R)
        w1T_lo = sb("w1T_lo", [P, DC, HID], F32R)
        w2T = sb("w2T", [P, HC, D])
        w2g = sb("w2g", [P, HC, D])
        w2g_hi = sb("w2g_hi", [P, HC, D], F32R)
        w2g_lo = sb("w2g_lo", [P, HC, D], F32R)
        wvT_hi = sb("wvT_hi", [P, DC, D + 2], F32R)
        wvT_lo = sb("wvT_lo", [P, DC, D + 2], F32R)
        mT_hi = sb("mT_hi", [P, DC, D], F32R)
        mT_lo = sb("mT_lo", [P, DC, D], F32R)
        bw2_half = sb("bw2_half", [P, D])
        small = sb("small", [P, 8])
        wkb, c2_col, bqbk = small[:, 0:DC], small[:, 2:2 + DC], small[:, 4:5]
        neg_half = sb("neg_half", [P, G])
        zero_row = sb("zero_row", [P, G])

        x_in = sb("x_in", [P, RING, G, D])
        adj_in = sb("adj_in", [P, RING, G, C])
        adjT = sb("adjT", [P, RING, G, C])
        hT = sb("hT", [P, G, C], F32R)
        count = sb("count", [P, G])
        be = sb("be", [P, G])
        be_hi = sb("be_hi", [P, G], F32R)
        be_lo = sb("be_lo", [P, G], F32R)
        hb_hi = sb("hb_hi", [P, G, C + 2], F32R)
        hb_lo = sb("hb_lo", [P, G, C + 2], F32R)
        s_mat = sb("s_mat", [P, RING, G, C + 2])
        dn_safe = sb("dn_safe", [P, G])
        dn_rec = sb("dn_rec", [P, G])
        dn = sb("dn", [P, RING, G])
        dn_deg = sb("dn_deg", [P, G])
        beta_term = sb("beta_term", [P, G, D])
        resid = sb("resid", [P, RING, G, D])
        sx_hi = sb("sx_hi", [P, G, DC, C], F32R)
        sx_lo = sb("sx_lo", [P, G, DC, C], F32R)
        h_pre = sb("h_pre", [P, G, HID])
        h_relu = sb("h_relu", [P, G, HID])
        h_norm = sb("h_norm", [P, G, HID])
        ln1_stats = sb("ln1_stats", [P, G, 6])
        ln1_mv = sb("ln1_mv", [P, G, 2])
        ln1_ve = sb("ln1_ve", [P, G])
        ln1_rstd = sb("ln1_rstd", [P, G])
        ln1_shift = sb("ln1_shift", [P, G])
        sh_hi = sb("sh_hi", [P, G, HC, C], F32R)
        sh_lo = sb("sh_lo", [P, G, HC, C], F32R)
        u = sb("u", [P, G, D])
        ln2_stats = sb("ln2_stats", [P, G, 6])
        ln2_mv = sb("ln2_mv", [P, G, 2])
        ln2_ve = sb("ln2_ve", [P, G])
        ln2_rstd = sb("ln2_rstd", [P, G])
        x1 = sb("x1", [P, G, D])
        x1_bv = sb("x1_bv", [P, G, D])
        x1T_hi = sb("x1T_hi", [P, DC, G, C], F32R)
        x1T_lo = sb("x1T_lo", [P, DC, G, C], F32R)
        zT_hi = sb("zT_hi", [P, DC, G, C], F32R)
        zT_lo = sb("zT_lo", [P, DC, G, C], F32R)
        val = sb("val", [P, G, D + 2])
        r_bias = sb("r_bias", [P, G])
        e_mat = sb("e_mat", [P, G, C])
        pT = sb("pT", [P, G, C])
        den_rec = sb("den_rec", [P, G])
        y_pre = sb("y_pre", [P, G, D])
        ln3_stats = sb("ln3_stats", [P, G, 6])
        ln3_mv = sb("ln3_mv", [P, G, 2])
        ln3_ve = sb("ln3_ve", [P, G])
        ln3_rstd = sb("ln3_rstd", [P, G])
        ln3_neg = sb("ln3_neg", [P, G])
        ln3_shift = sb("ln3_shift", [P, G])
        y = sb("y", [P, RING, G, D])

        bank = [ctx.enter_context(nc.psum_tensor(f"bank{n}", [P, 512], F32)) for n in range(8)]
        b_first = bank[0]
        b_out1 = bank[1:3]
        b_conv2 = bank[3:5]
        b_attn = bank[5]
        b_val = bank[6:8]

        x_landed = [sem(f"x_landed{s}") for s in range(RING)]
        adj_landed = [sem(f"adj_landed{s}") for s in range(RING)]
        y_stored = sem("y_stored")
        w1_landed, w2_landed, wqk_landed, wv_landed = sem("w1_landed"), sem("w2_landed"), sem("wqk_landed"), sem("wv_landed")
        rows_landed, cols_landed = sem("rows_landed"), sem("cols_landed")
        ident_ready, ident_zeroed, consts_set = sem("ident_ready"), sem("ident_zeroed"), sem("consts_set")
        setup_pe, setup_act, setup_dve, b2_halved = sem("setup_pe"), sem("setup_act"), sem("setup_dve"), sem("b2_halved")
        adjT_done, s_done, sx_g = sem("adjT_done"), sem("s_done"), sem("sx_g")
        out1_g, shT_g, out2_g = sem("out1_g"), sem("shT_g"), sem("out2_g")
        x1T_done, zT_done, val_g, scores_done, att_done = sem("x1T_done"), sem("zT_done"), sem("val_g"), sem("scores_done"), sem("att_done")
        adjT_copied, s_copied, sx_hi_ready = sem("adjT_copied"), sem("s_copied"), sem("sx_hi_ready")
        relu_g, sh_hi_g, x1T_hi_ready, zT_hi_ready = sem("relu_g"), sem("sh_hi_g"), sem("x1T_hi_ready"), sem("zT_hi_ready")
        h_norm_g, hb_hi_g = sem("h_norm_g"), sem("hb_hi_g")
        val_copied_g, exp_g, y_ready = sem("val_copied_g"), sem("exp_g"), sem("y_ready")
        hT_g, be_max, be_ready = sem("hT_g"), sem("be_max"), sem("be_ready")
        dn_clamped, dn_inverted, dn_ready = sem("dn_clamped"), sem("dn_inverted"), sem("dn_ready")
        sx_lo_ready, pre1_g, sh_lo_g = sem("sx_lo_ready"), sem("pre1_g"), sem("sh_lo_g")
        stats1_g, mv1_g, shift1 = sem("stats1_g"), sem("mv1_g"), sem("shift1")
        u_g, stats2_g, mv2_g, x1_ready = sem("u_g"), sem("stats2_g"), sem("mv2_g"), sem("x1_ready")
        x1T_lo_ready, zT_lo_ready, r_ready = sem("x1T_lo_ready"), sem("zT_lo_ready"), sem("r_ready")
        den_ready, y_pre_g, stats3_g, mv3_g = sem("den_ready"), sem("y_pre_g"), sem("stats3_g"), sem("mv3_g")
        w_hi_ready, w_lo_ready, be_hi_ready, be_lo_ready, hb_lo_ready = (
            sem("w_hi_ready"), sem("w_lo_ready"), sem("be_hi_ready"), sem("be_lo_ready"), sem("hb_lo_ready"))
        dn_deg_ready, beta_scaled, beta_biased, resid_ready = sem("dn_deg_ready"), sem("beta_scaled"), sem("beta_biased"), sem("resid_ready")
        ve1_g, ve2_g, ve3_g = sem("ve1_g"), sem("ve2_g"), sem("ve3_g")
        rstd1, rstd2, rstd3 = sem("rstd1"), sem("rstd2"), sem("rstd3")
        neg3, shift3, x1_bv_ready, pT_ready = sem("neg3"), sem("shift3"), sem("x1_bv_ready"), sem("pT_ready")

        J_W1, J_SMALL, J_MT, J_WV, J_W2, J_BW2 = 1, 3, 4, 5, 6, 8
        SETUP_ACT, SETUP_DVE = 9, 14

        block = ctx.enter_context(nc.Block())

        @block.sync
        def _(sp):
            def load_adj(p):
                wait(sp, adjT_done, p.back(RING).number + 1)
                sp.dma_start(adj_in[:, p.slot], adj_pairs[bass.ds(p.number, 1)].squeeze(0)).then_inc(adj_landed[p.slot], 16)

            def load_x(p):
                wait(sp, resid_ready, p.back(RING).number + 1)
                wait(sp, sx_g, G * p.back(RING).number + G)
                sp.dma_start(x_in[:, p.slot], x_pairs[bass.ds(p.number, 1)].squeeze(0)).then_inc(x_landed[p.slot], 16)

            load_adj(pair(0))
            sp.dma_start(w1_nat[:, :, :], w1.rearrange("(c p) d -> p c d", p=P)).then_inc(w1_landed, 16)
            sp.dma_start(w2_nat[:, :, :], w2.rearrange("(c p) d -> p c d", p=P)).then_inc(w2_landed, 16)

            def iteration(p):
                if p.back(-1).exists():
                    load_adj(p.back(-1))
                if p.exists():
                    load_x(p)
                last = p.back(4)
                if last.exists():
                    wait(sp, y_stored, 16 * last.number)
                    wait(sp, y_ready, G * last.number + G)
                    sp.dma_start(out_pairs[bass.ds(last.number, 1)].squeeze(0), y[:, last.slot]).then_inc(y_stored, 16)

            over_pairs(sp, iteration)
            sp.wait_ge(y_stored, 16 * PAIRS)

        @block.tensor
        def _(pe):
            def three_passes(psum, hi, lo, r_hi, r_lo, start, stop):
                pe.matmul(psum, hi, r_hi, start=start, stop=False)
                pe.matmul(psum, hi, r_lo, start=False, stop=False)
                return pe.matmul(psum, lo, r_hi, start=False, stop=stop)

            pe.wait_ge(ident_ready, 1)
            pe.wait_ge(w1_landed, 16)
            for dc in range(DC):
                for hc in range(HC):
                    last = pe.transpose(b_out1[dc][:, hc * P:(hc + 1) * P], w1_nat[:, hc, dc * P:(dc + 1) * P], ident[:, :])
                last.then_inc(setup_pe, 1)
            pe.wait_ge(wqk_landed, 32)
            pe.wait_ge(cols_landed, 64)
            for col, w, b in ((0, wk_nat, bq_col), (2, wq_nat, bk_col)):
                for dc in range(DC):
                    for oc in range(DC):
                        pe.matmul(b_attn[:, col + dc:col + dc + 1], w[:, oc, dc * P:(dc + 1) * P], b[:, oc:oc + 1],
                                  start=(oc == 0), stop=(oc == DC - 1))
            for oc in range(DC):
                last = pe.matmul(b_attn[:, 4:5], bq_col[:, oc:oc + 1].to_broadcast([P, P]), bk_col[:, oc:oc + 1],
                                 start=(oc == 0), stop=(oc == DC - 1))
            last.then_inc(setup_pe, 1)
            for kc in range(DC):
                for oc in range(DC):
                    last = pe.matmul(b_val[0][:, kc * D:(kc + 1) * D], wk_nat[:, oc, kc * P:(kc + 1) * P], wq_nat[:, oc, :],
                                     start=(oc == 0), stop=(oc == DC - 1))
            last.then_inc(setup_pe, 1)
            pe.wait_ge(wv_landed, 16)
            for dc in range(DC):
                for oc in range(DC):
                    last = pe.transpose(b_val[1][:, dc * D + oc * P:dc * D + (oc + 1) * P],
                                        wv_nat[:, oc, dc * P:(dc + 1) * P], ident[:, :])
            last.then_inc(setup_pe, 1)
            pe.wait_ge(w2_landed, 16)
            for hc in range(HC):
                for oc in range(DC):
                    last = pe.transpose(b_conv2[hc // 2][:, (hc % 2) * D + oc * P:(hc % 2) * D + (oc + 1) * P],
                                        w2_nat[:, oc, hc * P:(hc + 1) * P], ident[:, :])
                if hc % 2:
                    last.then_inc(setup_pe, 1)
            pe.wait_ge(setup_act, 8)
            for hc in range(HC):
                last = pe.matmul(b_first[:, 0:D], beta_col[:, hc:hc + 1].to_broadcast([P, P]), w2T[:, hc, :],
                                 start=(hc == 0), stop=(hc == HC - 1))
            last.then_inc(setup_pe, 1)
            pe.wait_ge(setup_act, SETUP_ACT)
            pe.wait_ge(setup_dve, SETUP_DVE)

            def adj_transposed(p):
                if p.exists():
                    wait(pe, adj_landed[p.slot], p.lap * 16 + 16)
                    wait(pe, sx_lo_ready, p.back(1).number + 1)
                    for g in range(G):
                        last = pe.transpose(b_first[:, g * C:(g + 1) * C], adj_in[:, p.slot, g, :], ident[:, :])
                    last.then_inc(adjT_done, 1)

            def node_matrix(p):
                if p.exists():
                    wait(pe, hT_g, G * p.number + G)
                    wait(pe, hb_hi_g, G * p.number + G)
                    wait(pe, w_lo_ready, p.number + 1)
                    wait(pe, hb_lo_ready, p.number + 1)
                    wait(pe, adjT_copied, p.number + 1)
                    for g in range(G):
                        dst = b_first[:, g * (C + 2):(g + 1) * (C + 2)]
                        pe.matmul(dst, hT[:, g, :], hb_hi[:, g, :], start=True, stop=False)
                        last = pe.matmul(dst, hT[:, g, :], hb_lo[:, g, :], start=False, stop=True)
                    last.then_inc(s_done, 1)

            def sx(p, g):
                if p.exists():
                    wait(pe, s_copied, p.number + 1)
                    wait(pe, x_landed[p.slot], p.lap * 16 + 16)
                    for dc in range(DC):
                        last = pe.matmul(b_first[:, (g * DC + dc) * C:(g * DC + dc + 1) * C],
                                         x_in[:, p.slot, g, dc * P:(dc + 1) * P], s_mat[:, p.slot, g, 0:C],
                                         start=True, stop=True)
                    last.then_inc(sx_g, 1)

            def out1(p, g):
                if p.exists():
                    wait(pe, sx_hi_ready, p.number + 1)
                    wait(pe, sx_lo_ready, p.number + 1)
                    wait(pe, pre1_g, G * p.back(1).number + g + 1)
                    for dc in range(DC):
                        last = three_passes(b_out1[g][:, :], sx_hi[:, g, dc, :], sx_lo[:, g, dc, :],
                                            w1T_hi[:, dc, :], w1T_lo[:, dc, :], dc == 0, dc == DC - 1)
                    last.then_inc(out1_g, 1)

            def sh(p, g):
                if p.exists():
                    wait(pe, h_norm_g, G * p.number + g + 1)
                    wait(pe, u_g, G * p.back(1).number + g + 1)
                    for hc in range(HC):
                        last = pe.matmul(b_conv2[g][:, hc * C:(hc + 1) * C], h_norm[:, g, hc * P:(hc + 1) * P],
                                         s_mat[:, p.slot, g, 0:C], start=True, stop=True)
                    last.then_inc(shT_g, 1)

            def out2(p, g):
                if p.exists():
                    wait(pe, sh_hi_g, G * p.number + g + 1)
                    wait(pe, sh_lo_g, G * p.number + g + 1)
                    for hc in range(HC):
                        last = three_passes(b_conv2[g][:, 0:D], sh_hi[:, g, hc, :], sh_lo[:, g, hc, :],
                                            w2g_hi[:, hc, :], w2g_lo[:, hc, :], hc == 0, hc == HC - 1)
                    last.then_inc(out2_g, 1)

            def x1_transposed(p):
                if p.exists():
                    wait(pe, x1_ready, p.number + 1)
                    wait(pe, exp_g, G * p.back(1).number + G)
                    for dc in range(DC):
                        for g in range(G):
                            last = pe.transpose(b_attn[:, (dc * G + g) * C:(dc * G + g + 1) * C],
                                                x1[:, g, dc * P:(dc + 1) * P], ident[:, :])
                    last.then_inc(x1T_done, 1)

            def attention(p):
                if p.exists():
                    wait(pe, pT_ready, p.number + 1)
                    wait(pe, val_copied_g, G * p.number + G)
                    for g in range(G):
                        last = pe.matmul(b_val[g][:, 0:D + 2], pT[:, g, :], val[:, g, :], start=True, stop=True)
                    last.then_inc(att_done, 1)

            def z_and_values(p):
                if p.exists():
                    wait(pe, x1T_hi_ready, p.number + 1)
                    wait(pe, x1T_lo_ready, p.number + 1)
                    for dc in range(DC):
                        for kc in range(DC):
                            last = three_passes(b_attn[:, dc * G * C:(dc + 1) * G * C],
                                                mT_hi[:, kc, dc * P:(dc + 1) * P], mT_lo[:, kc, dc * P:(dc + 1) * P],
                                                x1T_hi[:, kc, :, :], x1T_lo[:, kc, :, :], kc == 0, kc == DC - 1)
                    last.then_inc(zT_done, 1)
                    for g in range(G):
                        wait(pe, y_pre_g, G * p.back(1).number + g + 1)
                        for dc in range(DC):
                            last = three_passes(b_val[g][:, 0:D + 2], x1T_hi[:, dc, g, :], x1T_lo[:, dc, g, :],
                                                wvT_hi[:, dc, :], wvT_lo[:, dc, :], dc == 0, dc == DC - 1)
                        last.then_inc(val_g, 1)

            def scores(p):
                if p.exists():
                    wait(pe, zT_hi_ready, p.number + 1)
                    wait(pe, zT_lo_ready, p.number + 1)
                    for g in range(G):
                        for dc in range(DC):
                            last = three_passes(b_attn[:, g * C:(g + 1) * C], zT_hi[:, dc, g, :], zT_lo[:, dc, g, :],
                                                x1T_hi[:, dc, g, :], x1T_lo[:, dc, g, :], dc == 0, dc == DC - 1)
                    last.then_inc(scores_done, 1)

            def iteration(p):
                out1(p.back(2), 0)
                node_matrix(p.back(1))
                out1(p.back(2), 1)
                sx(p.back(1), 0)
                x1_transposed(p.back(3))
                sx(p.back(1), 1)
                attention(p.back(4))
                z_and_values(p.back(3))
                sh(p.back(2), 0)
                scores(p.back(3))
                sh(p.back(2), 1)
                out2(p.back(2), 0)
                adj_transposed(p)
                out2(p.back(2), 1)

            over_pairs(pe, iteration)

        @block.scalar
        def _(act):
            act.dma_start(wq_nat[:, :, :], wq_w.rearrange("(c p) d -> p c d", p=P)).then_inc(wqk_landed, 16)
            act.dma_start(wk_nat[:, :, :], wk_w.rearrange("(c p) d -> p c d", p=P)).then_inc(wqk_landed, 16)
            act.dma_start(wv_nat[:, :, :], wv_w.rearrange("(c p) d -> p c d", p=P)).then_inc(wv_landed, 16)
            act.dma_start(b1_rows[:, :], b1.partition_broadcast(P)).then_inc(rows_landed, 16)
            act.dma_start(b2_half[:, :], b2.partition_broadcast(P)).then_inc(rows_landed, 16)
            act.dma_start(bv_rows[:, :], wv_b.partition_broadcast(P)).then_inc(rows_landed, 16)

            for dc in range(DC):
                act.wait_ge(setup_pe, J_W1 + dc)
                act.activation(w1T_hi[:, dc, :], b_out1[dc][:, :], ACT.Copy).then_inc(setup_act, 1)
            act.wait_ge(setup_pe, J_SMALL)
            act.activation(small[:, 0:5], b_attn[:, 0:5], ACT.Copy).then_inc(setup_act, 1)
            act.wait_ge(setup_pe, J_MT)
            act.activation(mT_hi[:, :, :], b_val[0][:, :].rearrange("p (c d) -> p c d", c=DC), ACT.Copy).then_inc(setup_act, 1)
            act.wait_ge(setup_pe, J_WV)
            act.activation(wvT_hi[:, :, 0:D], b_val[1][:, :].rearrange("p (c d) -> p c d", c=DC), ACT.Copy).then_inc(setup_act, 1)
            act.wait_ge(setup_act, 3)
            act.activation(wvT_hi[:, :, D:D + 1], wkb.unsqueeze(2), ACT.Copy).then_inc(setup_act, 1)
            for j in range(2):
                act.wait_ge(setup_pe, J_W2 + j)
                act.activation(w2T[:, 2 * j:2 * j + 2, :], b_conv2[j][:, :].rearrange("p (c d) -> p c d", c=2),
                               ACT.Copy).then_inc(setup_act, 1)
            act.wait_ge(setup_dve, 9)
            act.activation(w2g_hi[:, :, :], w2g[:, :, :], ACT.Copy).then_inc(setup_act, 1)

            def copy_adjT(p):
                if p.exists():
                    wait(act, adjT_done, p.number + 1)
                    wait(act, pT_ready, p.back(RING).number + 1)
                    act.activation(adjT[:, p.slot], b_first[:, 0:G * C].rearrange("p (g c) -> p g c", g=G),
                                   ACT.Copy).then_inc(adjT_copied, 1)

            def be_hT_hi(p):
                if p.exists():
                    wait(act, be_hi_ready, p.number + 1)
                    wait(act, hT_g, G * p.number + G)
                    wait(act, s_done, p.back(1).number + 1)
                    for g in range(G):
                        act.activation(hb_hi[:, g, 0:C], hT[:, g, :].bitcast(F32), ACT.Copy,
                                       scale=be_hi[:, g:g + 1].bitcast(F32)).then_inc(hb_hi_g, 1)

            def copy_s(p):
                if p.exists():
                    wait(act, s_done, p.number + 1)
                    wait(act, shT_g, G * p.back(RING).number + G)
                    wait(act, resid_ready, p.back(RING).number + 1)
                    act.activation(s_mat[:, p.slot], b_first[:, 0:G * (C + 2)].rearrange("p (g c) -> p g c", g=G),
                                   ACT.Copy).then_inc(s_copied, 1)

            def split_sx(p):
                if p.exists():
                    wait(act, sx_g, G * p.number + G)
                    wait(act, out1_g, G * p.back(1).number + G)
                    act.activation(sx_hi[:, :, :, :], b_first[:, :].rearrange("p (g c n) -> p g c n", g=G, c=DC),
                                   ACT.Copy).then_inc(sx_hi_ready, 1)

            def relu(p, g):
                if p.exists():
                    wait(act, pre1_g, G * p.number + g + 1)
                    wait(act, h_norm_g, G * p.back(1).number + g + 1)
                    act.activation(h_relu[:, g, :], h_pre[:, g, :], ACT.Relu).then_inc(relu_g, 1)

            def normalise_h(p, g):
                if p.exists():
                    wait(act, shift1, p.number + 1)
                    wait(act, rstd1, p.number + 1)
                    wait(act, shT_g, G * p.back(1).number + g + 1)
                    act.activation(h_norm[:, g, :], h_relu[:, g, :], ACT.Identity, scale=ln1_rstd[:, g:g + 1],
                                   bias=ln1_shift[:, g:g + 1]).then_inc(h_norm_g, 1)

            def split_sh(p, g):
                if p.exists():
                    wait(act, shT_g, G * p.number + g + 1)
                    wait(act, out2_g, G * p.back(1).number + g + 1)
                    act.activation(sh_hi[:, g], b_conv2[g][:, :].rearrange("p (c n) -> p c n", c=HC),
                                   ACT.Copy).then_inc(sh_hi_g, 1)

            def split_x1T(p):
                if p.exists():
                    wait(act, x1T_done, p.number + 1)
                    wait(act, scores_done, p.back(1).number + 1)
                    act.activation(x1T_hi[:, :, :, :], b_attn[:, :].rearrange("p (c g n) -> p c g n", c=DC, g=G),
                                   ACT.Copy).then_inc(x1T_hi_ready, 1)

            def split_zT(p):
                if p.exists():
                    wait(act, zT_done, p.number + 1)
                    wait(act, scores_done, p.back(1).number + 1)
                    for dc in range(DC):
                        last = act.activation(zT_hi[:, dc].rearrange("p g n -> p (g n)"), b_attn[:, dc * G * C:(dc + 1) * G * C],
                                              ACT.Identity, bias=c2_col[:, dc:dc + 1])
                    last.then_inc(zT_hi_ready, 1)

            def copy_values(p):
                if p.exists():
                    for g in range(G):
                        wait(act, val_g, G * p.number + g + 1)
                        wait(act, att_done, p.back(1).number + 1)
                        act.activation(val[:, g, 0:D + 1], b_val[g][:, 0:D + 1], ACT.Copy).then_inc(val_copied_g, 1)

            def exponential(p):
                if p.exists():
                    wait(act, r_ready, p.number + 1)
                    wait(act, pT_ready, p.back(1).number + 1)
                    wait(act, scores_done, p.number + 1)
                    for g in range(G):
                        act.activation(e_mat[:, g, :], b_attn[:, g * C:(g + 1) * C], ACT.Exp,
                                       bias=r_bias[:, g:g + 1]).then_inc(exp_g, 1)

            def normalise_y(p):
                if p.exists():
                    wait(act, shift3, p.number + 1)
                    wait(act, rstd3, p.number + 1)
                    wait(act, y_stored, 16 * (p.number - 1))
                    for g in range(G):
                        act.activation(y[:, p.slot, g, :], y_pre[:, g, :], ACT.Identity, scale=ln3_rstd[:, g:g + 1],
                                       bias=ln3_shift[:, g:g + 1]).then_inc(y_ready, 1)

            def iteration(p):
                copy_s(p.back(1))
                relu(p.back(2), 0)
                split_x1T(p.back(3))
                relu(p.back(2), 1)
                split_sx(p.back(1))
                split_zT(p.back(3))
                normalise_h(p.back(2), 0)
                normalise_h(p.back(2), 1)
                copy_values(p.back(3))
                split_sh(p.back(2), 0)
                exponential(p.back(3))
                split_sh(p.back(2), 1)
                normalise_y(p.back(4))
                copy_adjT(p)
                be_hT_hi(p)

            over_pairs(act, iteration)

        @block.vector
        def _(dve):
            dve.wait_ge(rows_landed, 48)
            dve.tensor_scalar(b2_half[:, :], b2_half[:, :], 0.5, None, ALU.mult).then_inc(b2_halved, 1)
            for dc in range(DC):
                dve.wait_ge(setup_act, 1 + dc)
                dve.tensor_tensor(w1T_lo[:, dc, :], b_out1[dc][:, :], w1T_hi[:, dc, :].bitcast(F32),
                                  ALU.subtract).then_inc(setup_dve, 1)
            dve.wait_ge(setup_act, 4)
            dve.tensor_tensor(mT_lo[:, :, :], b_val[0][:, :].rearrange("p (c d) -> p c d", c=DC), mT_hi[:, :, :].bitcast(F32),
                              ALU.subtract).then_inc(setup_dve, 1)
            dve.wait_ge(setup_act, 5)
            dve.tensor_tensor(wvT_lo[:, :, 0:D], b_val[1][:, :].rearrange("p (c d) -> p c d", c=DC),
                              wvT_hi[:, :, 0:D].bitcast(F32), ALU.subtract).then_inc(setup_dve, 1)
            dve.wait_ge(setup_act, 6)
            dve.tensor_tensor(wvT_lo[:, :, D:D + 1], wkb.unsqueeze(2), wvT_hi[:, :, D:D + 1].bitcast(F32),
                              ALU.subtract).then_inc(setup_dve, 1)
            dve.wait_ge(cols_landed, 64)
            for hc in range(HC):
                dve.wait_ge(setup_act, 7 + hc // 2)
                dve.tensor_scalar(w2g[:, hc, :], b_conv2[hc // 2][:, (hc % 2) * D:(hc % 2 + 1) * D],
                                  gamma_col[:, hc:hc + 1], 0.5, ALU.mult, ALU.mult).then_inc(setup_dve, 1)
            dve.wait_ge(setup_act, 9)
            dve.tensor_tensor(w2g_lo[:, :, :], w2g[:, :, :], w2g_hi[:, :, :].bitcast(F32), ALU.subtract).then_inc(setup_dve, 1)
            dve.wait_ge(setup_pe, J_BW2)
            dve.tensor_scalar(bw2_half[:, :], b_first[:, 0:D], 0.5, None, ALU.mult).then_inc(setup_dve, 1)
            dve.wait_ge(consts_set, 3)
            for t in (wvT_hi, wvT_lo):
                dve.tensor_copy(t[:, :, D + 1:D + 2], zero_row[:, :].unsqueeze(2)).then_inc(setup_dve, 1)
            dve.tensor_copy(hb_hi[:, :, C + 1:C + 2], val[:, :, D + 1:D + 2]).then_inc(setup_dve, 1)
            dve.tensor_copy(hb_lo[:, :, C + 1:C + 2], zero_row[:, :].unsqueeze(2)).then_inc(setup_dve, 1)

            def incidence(p):
                if p.exists():
                    wait(dve, adjT_copied, p.number + 1)
                    wait(dve, s_done, p.back(1).number + 1)
                    wait(dve, be_lo_ready, p.back(1).number + 1)
                    for g in range(G):
                        dve.tensor_scalar(hT[:, g, :], adjT[:, p.slot, g, :], 0.0, None, ALU.not_equal, ALU.add,
                                          accum_out=count[:, g:g + 1]).then_inc(hT_g, 1)
                    wait(dve, hT_g, G * p.number + G)
                    dve.tensor_scalar(be[:, :], count[:, :], 1.0, None, ALU.max).then_inc(be_max, 1)
                    wait(dve, be_max, p.number + 1)
                    dve.reciprocal(be[:, :], be[:, :]).then_inc(be_ready, 1)

            def node_weights(p):
                if p.exists():
                    wait(dve, s_copied, p.number + 1)
                    sums = s_mat[:, p.slot, :, C]
                    dve.tensor_scalar(dn_safe[:, :], sums, TINY, None, ALU.max).then_inc(dn_clamped, 1)
                    wait(dve, dn_clamped, p.number + 1)
                    dve.reciprocal(dn_rec[:, :], dn_safe[:, :]).then_inc(dn_inverted, 1)
                    wait(dve, dn_inverted, p.number + 1)
                    wait(dve, resid_ready, p.back(RING).number + 1)
                    dve.scalar_tensor_tensor(dn[:, p.slot, :], sums, 0.0, dn_rec[:, :], ALU.is_gt,
                                             ALU.mult).then_inc(dn_ready, 1)

            def moments_of_first(p, src, src_g, stats, stats_g):
                if p.exists():
                    wait(dve, src_g, G * p.number + 1)
                    dve.bn_stats(stats[:, 0, :], src[:, 0, :]).then_inc(stats_g, 1)

            def moments(p, src, src_g, stats, stats_g, mv, mv_g, eps, ve, ve_g, taken):
                if p.exists():
                    wait(dve, taken, p.number)
                    wait(dve, stats_g, G * p.number + 1)
                    wait(dve, src_g, G * p.number + 2)
                    dve.bn_stats(stats[:, 1, :], src[:, 1, :]).then_inc(stats_g, 1)
                    dve.bn_aggr(mv[:, 0, :], stats[:, 0, :]).then_inc(mv_g, 1)
                    wait(dve, stats_g, G * p.number + 2)
                    wait(dve, mv_g, G * p.number + 1)
                    dve.tensor_scalar(ve[:, 0:1], mv[:, 0, 1:2], eps, None, ALU.add).then_inc(ve_g, 1)
                    dve.bn_aggr(mv[:, 1, :], stats[:, 1, :]).then_inc(mv_g, 1)
                    wait(dve, mv_g, G * p.number + 2)
                    dve.tensor_scalar(ve[:, 1:2], mv[:, 1, 1:2], eps, None, ALU.add).then_inc(ve_g, 1)

            ln1 = (h_relu, relu_g, ln1_stats, stats1_g)
            ln2 = (u, u_g, ln2_stats, stats2_g)
            ln3 = (y_pre, y_pre_g, ln3_stats, stats3_g)

            def split_sx(p):
                if p.exists():
                    wait(dve, sx_hi_ready, p.number + 1)
                    wait(dve, out1_g, G * p.back(1).number + G)
                    dve.tensor_tensor(sx_lo[:, :, :, :], b_first[:, :].rearrange("p (g c n) -> p g c n", g=G, c=DC),
                                      sx_hi[:, :, :, :].bitcast(F32), ALU.subtract).then_inc(sx_lo_ready, 1)

            def first_conv(p, g):
                if p.exists():
                    wait(dve, dn_ready, p.number + 1)
                    wait(dve, relu_g, G * p.back(1).number + g + 1)
                    wait(dve, out1_g, G * p.number + g + 1)
                    dve.scalar_tensor_tensor(h_pre[:, g, :], b_out1[g][:, :], dn[:, p.slot, g:g + 1], b1_rows[:, :],
                                             ALU.mult, ALU.add).then_inc(pre1_g, 1)

            def shift_h(p):
                if p.exists():
                    wait(dve, h_norm_g, G * p.back(1).number + G)
                    wait(dve, rstd1, p.number + 1)
                    dve.scalar_tensor_tensor(ln1_shift[:, :], ln1_mv[:, :, 0], -1.0, ln1_rstd[:, :], ALU.mult,
                                             ALU.mult).then_inc(shift1, 1)

            def split_sh(p, g):
                if p.exists():
                    wait(dve, sh_hi_g, G * p.number + g + 1)
                    wait(dve, out2_g, G * p.back(1).number + g + 1)
                    dve.tensor_tensor(sh_lo[:, g], b_conv2[g][:, :].rearrange("p (c n) -> p c n", c=HC),
                                      sh_hi[:, g].bitcast(F32), ALU.subtract).then_inc(sh_lo_g, 1)

            def second_conv(p, g):
                if p.exists():
                    wait(dve, resid_ready, p.number + 1)
                    wait(dve, x1_ready, p.back(1).number + 1)
                    wait(dve, out2_g, G * p.number + g + 1)
                    dve.scalar_tensor_tensor(u[:, g, :], b_conv2[g][:, 0:D], dn[:, p.slot, g:g + 1],
                                             resid[:, p.slot, g, :], ALU.mult, ALU.add).then_inc(u_g, 1)

            def normalise_x1(p):
                if p.exists():
                    wait(dve, x1T_done, p.back(1).number + 1)
                    wait(dve, x1_bv_ready, p.back(1).number + 1)
                    wait(dve, rstd2, p.number + 1)
                    for g in range(G):
                        last = dve.tensor_scalar(x1[:, g, :], u[:, g, :], ln2_mv[:, g, 0:1], ln2_rstd[:, g:g + 1],
                                                 ALU.subtract, ALU.mult)
                    last.then_inc(x1_ready, 1)

            def split_x1T(p):
                if p.exists():
                    wait(dve, scores_done, p.back(1).number + 1)
                    wait(dve, x1T_hi_ready, p.number + 1)
                    dve.tensor_tensor(x1T_lo[:, :, :, :], b_attn[:, :].rearrange("p (c g n) -> p c g n", c=DC, g=G),
                                      x1T_hi[:, :, :, :].bitcast(F32), ALU.subtract).then_inc(x1T_lo_ready, 1)

            def split_zT(p):
                if p.exists():
                    wait(dve, zT_hi_ready, p.number + 1)
                    for dc in range(DC):
                        last = dve.scalar_tensor_tensor(
                            zT_lo[:, dc].rearrange("p g n -> p (g n)"), b_attn[:, dc * G * C:(dc + 1) * G * C],
                            c2_col[:, dc:dc + 1], zT_hi[:, dc].rearrange("p g n -> p (g n)").bitcast(F32),
                            ALU.add, ALU.subtract)
                    last.then_inc(zT_lo_ready, 1)

            def score_bias(p):
                if p.exists():
                    wait(dve, exp_g, G * p.back(1).number + G)
                    wait(dve, val_copied_g, G * p.number + G)
                    dve.tensor_scalar(r_bias[:, :], val[:, :, D], bqbk, None, ALU.add).then_inc(r_ready, 1)

            def attention(p):
                if p.exists():
                    wait(dve, att_done, p.number + 1)
                    for g in range(G):
                        dve.reciprocal(den_rec[:, g:g + 1], b_val[g][:, D + 1:D + 2]).then_inc(den_ready, 1)
                    wait(dve, x1_bv_ready, p.number + 1)
                    wait(dve, y_ready, G * p.back(1).number + G)
                    for g in range(G):
                        wait(dve, den_ready, G * p.number + g + 1)
                        dve.scalar_tensor_tensor(y_pre[:, g, :], b_val[g][:, 0:D], den_rec[:, g:g + 1], x1_bv[:, g, :],
                                                 ALU.mult, ALU.add).then_inc(y_pre_g, 1)

            def iteration(p):
                moments_of_first(p.back(3), *ln2)
                moments(p.back(3), *ln2, ln2_mv, mv2_g, EPS / 4, ln2_ve, ve2_g, rstd2)
                first_conv(p.back(2), 0)
                normalise_x1(p.back(3))
                node_weights(p.back(1))
                first_conv(p.back(2), 1)
                moments_of_first(p.back(2), *ln1)
                split_x1T(p.back(3))
                moments(p.back(2), *ln1, ln1_mv, mv1_g, EPS, ln1_ve, ve1_g, rstd1)
                attention(p.back(4))
                shift_h(p.back(2))
                split_zT(p.back(3))
                moments_of_first(p.back(4), *ln3)
                moments(p.back(4), *ln3, ln3_mv, mv3_g, EPS, ln3_ve, ve3_g, shift3)
                score_bias(p.back(3))
                split_sh(p.back(2), 0)
                split_sx(p.back(1))
                split_sh(p.back(2), 1)
                second_conv(p.back(2), 0)
                incidence(p)
                second_conv(p.back(2), 1)

            over_pairs(dve, iteration)

        @block.gpsimd
        def _(pool):
            pool.memset(ident[:, :], 0.0).then_inc(ident_zeroed, 1)
            for t, v in ((gamma_col, gamma), (beta_col, beta)):
                pool.dma_start(t[:, :], v.rearrange("(c p) -> p c", p=P), allow_slow_non_contiguous=True).then_inc(cols_landed, 16)
            for t, v in ((bq_col, wq_b), (bk_col, wk_b)):
                pool.dma_start(t[:, :], v.rearrange("(c p) -> p c", p=P), allow_slow_non_contiguous=True).then_inc(cols_landed, 16)
            pool.wait_ge(ident_zeroed, 1)
            pool.affine_select(out=ident[:, :], in_=ident[:, :], compare_op=ALU.not_equal, fill=1.0, base=0,
                               pattern=[[-1, P]], channel_multiplier=1).then_inc(ident_ready, 1)
            pool.memset(neg_half[:, :], -0.5).then_inc(consts_set, 1)
            pool.memset(zero_row[:, :], 0.0).then_inc(consts_set, 1)
            pool.memset(val[:, :, D + 1:D + 2], 1.0).then_inc(consts_set, 1)

            def edge_weights(p):
                if p.exists():
                    wait(pool, adjT_copied, p.number + 1)
                    wait(pool, s_done, p.back(1).number + 1)
                    w_row = adjT[:, p.slot, :, 0:1]
                    pool.tensor_tensor(hb_hi[:, :, C:C + 1], w_row, zero_row[:, :].unsqueeze(2), ALU.add).then_inc(w_hi_ready, 1)
                    wait(pool, hb_hi_g, G * p.back(1).number + G)
                    wait(pool, be_ready, p.number + 1)
                    pool.tensor_tensor(be_hi[:, :], be[:, :], zero_row[:, :], ALU.add).then_inc(be_hi_ready, 1)
                    wait(pool, be_hi_ready, p.number + 1)
                    pool.tensor_tensor(be_lo[:, :], be[:, :], be_hi[:, :].bitcast(F32), ALU.subtract).then_inc(be_lo_ready, 1)
                    wait(pool, hT_g, G * p.number + G)
                    wait(pool, be_lo_ready, p.number + 1)
                    pool.tensor_tensor(hb_lo[:, :, 0:C], hT[:, :, :].bitcast(F32),
                                       be_lo[:, :].bitcast(F32).unsqueeze(2).to_broadcast([P, G, C]),
                                       ALU.mult).then_inc(hb_lo_ready, 1)
                    wait(pool, w_hi_ready, p.number + 1)
                    pool.tensor_tensor(hb_lo[:, :, C:C + 1], w_row, hb_hi[:, :, C:C + 1].bitcast(F32),
                                       ALU.subtract).then_inc(w_lo_ready, 1)

            def rsqrt(p, ve, ve_g, rstd, rstd_done):
                wait(pool, ve_g, G * p.number + G)
                pool.tensor_tensor(rstd[:, :], ve[:, :], neg_half[:, :], ALU.pow).then_inc(rstd_done, 1)

            pool.wait_ge(consts_set, 3)
            pool.wait_ge(setup_dve, SETUP_DVE)
            pool.wait_ge(b2_halved, 1)

            def residual(p):
                if p.exists():
                    wait(pool, dn_ready, p.number + 1)
                    pool.tensor_tensor(dn_deg[:, :], dn[:, p.slot, :], s_mat[:, p.slot, :, C + 1],
                                       ALU.mult).then_inc(dn_deg_ready, 1)
                    wait(pool, dn_deg_ready, p.number + 1)
                    pool.tensor_tensor(beta_term[:, :, :], bw2_half[:, :].unsqueeze(1).to_broadcast([P, G, D]),
                                       dn_deg[:, :].unsqueeze(2).to_broadcast([P, G, D]), ALU.mult).then_inc(beta_scaled, 1)
                    wait(pool, beta_scaled, p.number + 1)
                    pool.tensor_tensor(beta_term[:, :, :], beta_term[:, :, :],
                                       b2_half[:, :].unsqueeze(1).to_broadcast([P, G, D]), ALU.add).then_inc(beta_biased, 1)
                    wait(pool, x_landed[p.slot], p.lap * 16 + 16)
                    wait(pool, u_g, G * p.back(RING).number + G)
                    wait(pool, beta_biased, p.number + 1)
                    pool.tensor_tensor(resid[:, p.slot], x_in[:, p.slot], beta_term[:, :, :], ALU.add).then_inc(resid_ready, 1)

            def rstd_of_h(p):
                if p.exists():
                    wait(pool, h_norm_g, G * p.back(1).number + G)
                    rsqrt(p, ln1_ve, ve1_g, ln1_rstd, rstd1)

            def rstd_of_x1(p):
                if p.exists():
                    wait(pool, x1_ready, p.back(1).number + 1)
                    rsqrt(p, ln2_ve, ve2_g, ln2_rstd, rstd2)

            def rstd_of_y(p):
                if p.exists():
                    wait(pool, y_ready, G * p.back(1).number + G)
                    rsqrt(p, ln3_ve, ve3_g, ln3_rstd, rstd3)
                    pool.tensor_tensor(ln3_neg[:, :], zero_row[:, :], ln3_mv[:, :, 0], ALU.subtract).then_inc(neg3, 1)
                    wait(pool, rstd3, p.number + 1)
                    wait(pool, neg3, p.number + 1)
                    pool.tensor_tensor(ln3_shift[:, :], ln3_neg[:, :], ln3_rstd[:, :], ALU.mult).then_inc(shift3, 1)

            def add_value_bias(p):
                if p.exists():
                    wait(pool, x1_ready, p.number + 1)
                    wait(pool, y_pre_g, G * p.back(1).number + G)
                    pool.tensor_tensor(x1_bv[:, :, :], x1[:, :, :], bv_rows[:, :].unsqueeze(1).to_broadcast([P, G, D]),
                                       ALU.add).then_inc(x1_bv_ready, 1)

            def weigh(p):
                if p.exists():
                    wait(pool, att_done, p.back(1).number + 1)
                    wait(pool, exp_g, G * p.number + G)
                    pool.tensor_tensor(pT[:, :, :], adjT[:, p.slot], e_mat[:, :, :], ALU.mult).then_inc(pT_ready, 1)

            def iteration(p):
                rstd_of_x1(p.back(3))
                residual(p.back(1))
                rstd_of_h(p.back(2))
                add_value_bias(p.back(3))
                rstd_of_y(p.back(4))
                weigh(p.back(3))
                edge_weights(p)

            over_pairs(pool, iteration)


_INS = ['x', 'adj', 'L0_gnn_W1', 'L0_gnn_b1', 'L0_gnn_gamma', 'L0_gnn_beta', 'L0_gnn_W2', 'L0_gnn_b2',
        'L1_gnn_Wq_w', 'L1_gnn_Wq_b', 'L1_gnn_Wk_w', 'L1_gnn_Wk_b', 'L1_gnn_Wv_w', 'L1_gnn_Wv_b']


def kernel(**inputs):
    import numpy as _np
    import concourse.bacc as _bacc
    from concourse import mybir as _mybir
    from concourse.bass_utils import run_bass_kernel_spmd as _run

    nc = _bacc.Bacc("TRN2", target_bir_lowering=False, num_devices=1)
    arrays, args = {}, []
    for name in _INS:
        a = _np.ascontiguousarray(inputs[name])
        arrays[f"in_{name}_dram"] = a
        args.append(nc.dram_tensor(f"in_{name}_dram", a.shape, _mybir.dt.from_np(a.dtype), kind="ExternalInput").ap())
    shape = arrays["in_x_dram"].shape
    args.append(nc.dram_tensor("out_dram", shape, _mybir.dt.float32, kind="ExternalOutput").ap())
    build(nc, *args)
    r = _run(nc, [arrays], core_ids=[0])
    return r.results[0]["out_dram"]
```

```python
from contextlib import ExitStack

import concourse.bass as bass
from concourse import mybir

ALU = mybir.AluOpType
ACT = mybir.ActivationFunctionType
F32 = mybir.dt.float32
F32R = mybir.dt.float32r

P = 128
G = 2
RING = 4
Y_RING = 2
EPS = 1e-5
TINY = 1.1754944e-38


class Pair:

    def __init__(self, lap, slot, pairs):
        self.lap, self.slot, self.pairs = lap, slot, pairs

    @property
    def number(self):
        return self.lap * RING + self.slot

    def back(self, n):
        moved = self.slot - n
        return Pair(self.lap + moved // RING, moved % RING, self.pairs)

    @property
    def clamped(self):
        return self.number if not isinstance(self.lap, int) else min(self.number, self.pairs - 1)

    def exists(self):
        return not isinstance(self.lap, int) or 0 <= self.number < self.pairs


def wait(eng, sem, value):
    if not isinstance(value, int) or value > 0:
        eng.wait_ge(sem, value)


def build(nc, x, adj, w1, b1, gamma, beta, w2, b2, wq_w, wq_b, wk_w, wk_b, wv_w, wv_b, out):
    N, C, D = x.shape
    HID = w1.shape[0]
    DC, HC = D // P, HID // P
    PAIRS = N // G
    assert C == P and N % (G * RING) == 0

    x_pairs = x.rearrange("(k g) c d -> k c g d", g=G)
    adj_pairs = adj.rearrange("(k g) c e -> k c g e", g=G)
    out_pairs = out.rearrange("(k g) c d -> k c g d", g=G)

    LAG = 5
    FIRST_AHEAD = 2
    ATT_BEHIND = 3
    ADJ_AHEAD, X_AHEAD = 2, 1
    LOOP_FROM = 2
    LOOP_TO = (PAIRS - ADJ_AHEAD) // RING

    def pair(k):
        return Pair(k // RING, k % RING, PAIRS)

    def over_pairs(eng, iteration, start=0, end=PAIRS + LAG):
        for k in range(start, LOOP_FROM * RING):
            iteration(pair(k))
        with eng.Fori(LOOP_FROM, LOOP_TO) as lap:
            for slot in range(RING):
                iteration(Pair(lap, slot, PAIRS))
        for k in range(LOOP_TO * RING, end):
            iteration(pair(k))

    with ExitStack() as ctx:
        def sb(name, shape, dt=F32):
            return ctx.enter_context(nc.sbuf_tensor(name, shape, dt))

        def sem(name):
            return ctx.enter_context(nc.semaphore(name))

        ident = sb("ident", [P, P])
        w1_nat = sb("w1_nat", [P, HC, D])
        w2_nat = sb("w2_nat", [P, DC, HID])
        wq_nat = sb("wq_nat", [P, DC, D])
        wk_nat = sb("wk_nat", [P, DC, D])
        wv_nat = sb("wv_nat", [P, DC, D])
        b1_rows = sb("b1_rows", [P, HID])
        b2_half = sb("b2_half", [P, D])
        bv_rows = sb("bv_rows", [P, D])
        gamma_col = sb("gamma_col", [P, HC])
        beta_col = sb("beta_col", [P, HC])
        bq_col = sb("bq_col", [P, DC])
        bk_col = sb("bk_col", [P, DC])
        w1T_hi = sb("w1T_hi", [P, DC, HID], F32R)
        w1T_lo = sb("w1T_lo", [P, DC, HID], F32R)
        w2T = sb("w2T", [P, HC, D])
        w2g = sb("w2g", [P, HC, D])
        w2g_hi = sb("w2g_hi", [P, HC, D], F32R)
        w2g_lo = sb("w2g_lo", [P, HC, D], F32R)
        wvT_hi = sb("wvT_hi", [P, DC, D + 2], F32R)
        wvT_lo = sb("wvT_lo", [P, DC, D + 2], F32R)
        mT_hi = sb("mT_hi", [P, DC, D], F32R)
        mT_lo = sb("mT_lo", [P, DC, D], F32R)
        bw2_half = sb("bw2_half", [P, D])
        small = sb("small", [P, 8])
        wkb, c2_col, bqbk = small[:, 0:DC], small[:, 2:2 + DC], small[:, 4:5]
        neg_half = sb("neg_half", [P, G])
        zero_row = sb("zero_row", [P, G])

        x_in = sb("x_in", [P, RING, G, D])
        adj_in = sb("adj_in", [P, RING, G, C])
        adjT = sb("adjT", [P, RING, G, C])
        hT = sb("hT", [P, G, C])
        count = sb("count", [P, G])
        be = sb("be", [P, G])
        hb = sb("hb", [P, G, C + 2])
        s_mat = sb("s_mat", [P, RING, G, C + 2])
        dn_safe = sb("dn_safe", [P, G])
        dn_rec = sb("dn_rec", [P, G])
        dn = sb("dn", [P, RING, G])
        dn_deg = sb("dn_deg", [P, G])
        beta_term = sb("beta_term", [P, G, D])
        resid = sb("resid", [P, RING, G, D])
        sx_hi = sb("sx_hi", [P, G, DC, C], F32R)
        sx_lo = sb("sx_lo", [P, G, DC, C], F32R)
        h_pre = sb("h_pre", [P, G, HID])
        h_relu = sb("h_relu", [P, G, HID])
        h_norm = sb("h_norm", [P, G, HID])
        ln1_stats = sb("ln1_stats", [P, G, 6])
        ln1_mv = sb("ln1_mv", [P, G, 2])
        ln1_ve = sb("ln1_ve", [P, G])
        ln1_rstd = sb("ln1_rstd", [P, G])
        ln1_shift = sb("ln1_shift", [P, G])
        sh_hi = sb("sh_hi", [P, G, HC, C], F32R)
        sh_lo = sb("sh_lo", [P, G, HC, C], F32R)
        u = sb("u", [P, G, D])
        ln2_stats = sb("ln2_stats", [P, G, 6])
        ln2_mv = sb("ln2_mv", [P, G, 2])
        ln2_ve = sb("ln2_ve", [P, G])
        ln2_rstd = sb("ln2_rstd", [P, G])
        x1 = sb("x1", [P, G, D])
        x1_bv = sb("x1_bv", [P, G, D])
        x1T = sb("x1T", [P, DC, G, C])
        x1T_hi = sb("x1T_hi", [P, DC, G, C], F32R)
        x1T_lo = sb("x1T_lo", [P, DC, G, C], F32R)
        zT = sb("zT", [P, DC, G, C])
        val = sb("val", [P, G, D + 2])
        r_bias = sb("r_bias", [P, G])
        e_mat = sb("e_mat", [P, G, C])
        pT = sb("pT", [P, G, C])
        den_rec = sb("den_rec", [P, G])
        y_pre = sb("y_pre", [P, G, D])
        ln3_stats = sb("ln3_stats", [P, G, 6])
        ln3_mv = sb("ln3_mv", [P, G, 2])
        ln3_ve = sb("ln3_ve", [P, G])
        ln3_rstd = sb("ln3_rstd", [P, G])
        ln3_neg = sb("ln3_neg", [P, G])
        ln3_shift = sb("ln3_shift", [P, G])
        y = sb("y", [P, Y_RING, G, D])

        bank = [ctx.enter_context(nc.psum_tensor(f"bank{n}", [P, 512], F32)) for n in range(8)]
        b_first = bank[0]
        b_out1 = bank[1:3]
        b_conv2 = bank[3:5]
        b_attn = bank[5]
        b_val = bank[6:8]
        b_att = b_out1

        x_landed = [sem(f"x_landed{s}") for s in range(RING)]
        adj_landed = [sem(f"adj_landed{s}") for s in range(RING)]
        y_stored = [sem(f"y_stored{s}") for s in range(Y_RING)]
        w1_landed, w2_landed, wqk_landed, wv_landed = (
            sem(n) for n in ("w1_landed", "w2_landed", "wqk_landed", "wv_landed"))
        b1_landed, b2_landed, bv_landed = sem("b1_landed"), sem("b2_landed"), sem("bv_landed")
        gamma_landed, beta_landed, bqk_landed = sem("gamma_landed"), sem("beta_landed"), sem("bqk_landed")
        ident_ready, ident_zeroed, consts_set = sem("ident_ready"), sem("ident_zeroed"), sem("consts_set")
        w1T_done, w2T_done, bw2_done, mT_done, small_done, wvT_done = (
            sem(n) for n in ("w1T_done", "w2T_done", "bw2_done", "mT_done", "small_done", "wvT_done"))
        w1T_hi_ready, w2T_ready, w2g_hi_ready, mT_hi_ready, small_ready, wvT_hi_ready = (
            sem(n) for n in ("w1T_hi_ready", "w2T_ready", "w2g_hi_ready", "mT_hi_ready", "small_ready", "wvT_hi_ready"))
        w1T_lo_ready, w2g_ready, w2g_lo_ready, bw2_ready, mT_lo_ready, wvT_lo_ready, b2_halved = (
            sem(n) for n in ("w1T_lo_ready", "w2g_ready", "w2g_lo_ready", "bw2_ready", "mT_lo_ready", "wvT_lo_ready",
                             "b2_halved"))

        def per_graph(name):
            return [sem(f"{name}_g{g}") for g in range(G)]

        adjT_done, s_done, x1T_done, zT_done = sem("adjT_done"), sem("s_done"), sem("x1T_done"), sem("zT_done")
        val_done, scores_done, att_done = sem("val_done"), sem("scores_done"), sem("att_done")
        sx_done, out1_done, shT_done, out2_done = (
            per_graph(n) for n in ("sx_done", "out1_done", "shT_done", "out2_done"))
        adjT_copied, s_copied, sx_hi_ready = sem("adjT_copied"), sem("s_copied"), sem("sx_hi_ready")
        relu_done, h_ready, sh_hi_ready = per_graph("relu"), per_graph("h"), per_graph("sh_hi")
        x1T_hi_ready, x1T_copied, zT_ready = sem("x1T_hi_ready"), sem("x1T_copied"), sem("zT_ready")
        val_copied, exp_done, y_ready = sem("val_copied"), sem("exp_done"), sem("y_ready")
        hT_ready, be_clamped, be_ready = per_graph("hT"), sem("be_clamped"), sem("be_ready")
        dn_clamped, dn_inverted, dn_ready = sem("dn_clamped"), sem("dn_inverted"), sem("dn_ready")
        sx_lo_ready, pre1_done, sh_lo_ready = sem("sx_lo_ready"), per_graph("pre1"), per_graph("sh_lo")
        u_ready, x1_ready, x1T_lo_ready = per_graph("u"), sem("x1_ready"), sem("x1T_lo_ready")
        r_ready, den_ready, y_pre_ready = sem("r_ready"), per_graph("den"), per_graph("y_pre")
        shift1 = sem("shift1")
        stats1, stats2, stats3 = per_graph("stats1"), per_graph("stats2"), per_graph("stats3")
        mv1, mv2, mv3, ve1, ve2, ve3 = (sem(n) for n in ("mv1", "mv2", "mv3", "ve1", "ve2", "ve3"))
        w_ready, hb_ready = sem("w_ready"), sem("hb_ready")
        dn_deg_ready, beta_scaled, beta_biased, resid_ready = (
            sem("dn_deg_ready"), sem("beta_scaled"), sem("beta_biased"), sem("resid_ready"))
        rstd1, rstd2, rstd3, neg3, shift3 = (sem(n) for n in ("rstd1", "rstd2", "rstd3", "neg3", "shift3"))
        x1_bv_ready, pT_ready = sem("x1_bv_ready"), sem("pT_ready")

        block = ctx.enter_context(nc.Block())

        @block.sync
        def _(sp):
            def load_adj(p):
                wait(sp, adjT_done, p.back(RING).number + 1)
                sp.dma_start(adj_in[:, p.slot],
                             adj_pairs[bass.ds(p.number, 1)].squeeze(0)).then_inc(adj_landed[p.slot], 16)

            def load_x(p):
                wait(sp, resid_ready, p.back(RING).number + 1)
                for g in range(G):
                    wait(sp, sx_done[g], p.back(RING).number + 1)
                sp.dma_start(x_in[:, p.slot],
                             x_pairs[bass.ds(p.number, 1)].squeeze(0)).then_inc(x_landed[p.slot], 16)

            def store_y(p):
                slot = p.slot % Y_RING
                wait(sp, y_ready, p.number + 1)
                sp.dma_start(out_pairs[bass.ds(p.number, 1)].squeeze(0), y[:, slot]).then_inc(y_stored[slot], 16)

            def iteration(p):
                if p.back(-ADJ_AHEAD).exists():
                    load_adj(p.back(-ADJ_AHEAD))
                if p.back(LAG).exists():
                    store_y(p.back(LAG))
                if p.back(-X_AHEAD).exists():
                    load_x(p.back(-X_AHEAD))

            load_adj(pair(0))
            sp.dma_start(w1_nat[:, :, :], w1.rearrange("(c p) d -> p c d", p=P)).then_inc(w1_landed, 16)
            sp.dma_start(w2_nat[:, :, :], w2.rearrange("(c p) d -> p c d", p=P)).then_inc(w2_landed, 16)
            load_x(pair(0))
            load_adj(pair(1))
            sp.dma_start(b1_rows[:, :], b1.partition_broadcast(P)).then_inc(b1_landed, 16)
            sp.dma_start(wq_nat[:, :, :], wq_w.rearrange("(c p) d -> p c d", p=P)).then_inc(wqk_landed, 16)
            sp.dma_start(wk_nat[:, :, :], wk_w.rearrange("(c p) d -> p c d", p=P)).then_inc(wqk_landed, 16)
            sp.dma_start(b2_half[:, :], b2.partition_broadcast(P)).then_inc(b2_landed, 16)
            load_x(pair(1))
            sp.dma_start(wv_nat[:, :, :], wv_w.rearrange("(c p) d -> p c d", p=P)).then_inc(wv_landed, 16)
            sp.dma_start(bv_rows[:, :], wv_b.partition_broadcast(P)).then_inc(bv_landed, 16)
            load_adj(pair(2))
            over_pairs(sp, iteration, start=1)
            for slot in range(Y_RING):
                sp.wait_ge(y_stored[slot], 16 * (PAIRS // Y_RING))

        @block.tensor
        def _(pe):
            def three_passes(psum, hi, lo, r_hi, r_lo, start, stop):
                pe.matmul(psum, hi, r_hi, start=start, stop=False)
                pe.matmul(psum, hi, r_lo, start=False, stop=False)
                return pe.matmul(psum, lo, r_hi, start=False, stop=stop)

            def w1_transposed():
                pe.wait_ge(w1_landed, 16)
                for dc in range(DC):
                    for hc in range(HC):
                        last = pe.transpose(b_out1[dc][:, hc * P:(hc + 1) * P], w1_nat[:, hc, dc * P:(dc + 1) * P],
                                            ident[:, :])
                    last.then_inc(w1T_done, 1)

            def w2_transposed():
                pe.wait_ge(w2_landed, 16)
                for hc in range(HC):
                    for oc in range(DC):
                        last = pe.transpose(b_conv2[hc // 2][:, (hc % 2) * D + oc * P:(hc % 2) * D + (oc + 1) * P],
                                            w2_nat[:, oc, hc * P:(hc + 1) * P], ident[:, :])
                    if hc % 2:
                        last.then_inc(w2T_done, 1)

            def beta_w2():
                pe.wait_ge(beta_landed, 16)
                pe.wait_ge(w2T_ready, 2)
                for hc in range(HC):
                    last = pe.matmul(b_attn[:, 0:D], beta_col[:, hc:hc + 1].to_broadcast([P, P]), w2T[:, hc, :],
                                     start=(hc == 0), stop=(hc == HC - 1))
                last.then_inc(bw2_done, 1)

            def m_transposed():
                pe.wait_ge(wqk_landed, 32)
                for kc in range(DC):
                    for oc in range(DC):
                        last = pe.matmul(b_val[0][:, kc * D:(kc + 1) * D], wk_nat[:, oc, kc * P:(kc + 1) * P],
                                         wq_nat[:, oc, :], start=(oc == 0), stop=(oc == DC - 1))
                last.then_inc(mT_done, 1)

            def bias_products():
                pe.wait_ge(bw2_ready, 1)
                pe.wait_ge(bqk_landed, 32)
                for col, w, b in ((0, wk_nat, bq_col), (2, wq_nat, bk_col)):
                    for dc in range(DC):
                        for oc in range(DC):
                            pe.matmul(b_attn[:, col + dc:col + dc + 1], w[:, oc, dc * P:(dc + 1) * P], b[:, oc:oc + 1],
                                      start=(oc == 0), stop=(oc == DC - 1))
                for oc in range(DC):
                    last = pe.matmul(b_attn[:, 4:5], bq_col[:, oc:oc + 1].to_broadcast([P, P]), bk_col[:, oc:oc + 1],
                                     start=(oc == 0), stop=(oc == DC - 1))
                last.then_inc(small_done, 1)

            def wv_transposed():
                pe.wait_ge(wv_landed, 16)
                for dc in range(DC):
                    for oc in range(DC):
                        last = pe.transpose(b_val[1][:, dc * D + oc * P:dc * D + (oc + 1) * P],
                                            wv_nat[:, oc, dc * P:(dc + 1) * P], ident[:, :])
                last.then_inc(wvT_done, 1)

            def adj_transposed(p):
                if p.exists():
                    wait(pe, adj_landed[p.slot], p.lap * 16 + 16)
                    wait(pe, sx_lo_ready, p.back(1).number + 1)
                    for g in range(G):
                        last = pe.transpose(b_first[:, g * C:(g + 1) * C], adj_in[:, p.slot, g, :], ident[:, :])
                    last.then_inc(adjT_done, 1)

            def node_matrix(p):
                if p.exists():
                    wait(pe, w_ready, p.number + 1)
                    wait(pe, hb_ready, p.number + 1)
                    wait(pe, adjT_copied, p.number + 1)
                    for g in range(G):
                        wait(pe, hT_ready[g], p.number + 1)
                        last = pe.matmul(b_first[:, g * (C + 2):(g + 1) * (C + 2)], hT[:, g, :], hb[:, g, :],
                                         start=True, stop=True)
                    last.then_inc(s_done, 1)

            def sx(p, g):
                if p.exists():
                    wait(pe, s_copied, p.number + 1)
                    wait(pe, x_landed[p.slot], p.lap * 16 + 16)
                    for dc in range(DC):
                        last = pe.matmul(b_first[:, (g * DC + dc) * C:(g * DC + dc + 1) * C],
                                         x_in[:, p.slot, g, dc * P:(dc + 1) * P], s_mat[:, p.slot, g, 0:C],
                                         start=True, stop=True)
                    last.then_inc(sx_done[g], 1)

            def out1(p, g):
                if p.exists():
                    wait(pe, sx_hi_ready, p.number + 1)
                    wait(pe, sx_lo_ready, p.number + 1)
                    wait(pe, pre1_done[g], p.back(1).number + 1)
                    wait(pe, y_pre_ready[g], p.back(ATT_BEHIND).clamped + 1)
                    for dc in range(DC):
                        last = three_passes(b_out1[g][:, :], sx_hi[:, g, dc, :], sx_lo[:, g, dc, :],
                                            w1T_hi[:, dc, :], w1T_lo[:, dc, :], dc == 0, dc == DC - 1)
                    last.then_inc(out1_done[g], 1)

            def sh(p, g):
                if p.exists():
                    wait(pe, h_ready[g], p.number + 1)
                    wait(pe, u_ready[g], p.back(1).number + 1)
                    for hc in range(HC):
                        last = pe.matmul(b_conv2[g][:, hc * C:(hc + 1) * C], h_norm[:, g, hc * P:(hc + 1) * P],
                                         s_mat[:, p.slot, g, 0:C], start=True, stop=True)
                    last.then_inc(shT_done[g], 1)

            def out2(p, g):
                if p.exists():
                    wait(pe, sh_hi_ready[g], p.number + 1)
                    wait(pe, sh_lo_ready[g], p.number + 1)
                    for hc in range(HC):
                        last = three_passes(b_conv2[g][:, 0:D], sh_hi[:, g, hc, :], sh_lo[:, g, hc, :],
                                            w2g_hi[:, hc, :], w2g_lo[:, hc, :], hc == 0, hc == HC - 1)
                    last.then_inc(out2_done[g], 1)

            def x1_transposed(p):
                if p.exists():
                    wait(pe, x1_ready, p.number + 1)
                    wait(pe, exp_done, p.back(1).number + 1)
                    for dc in range(DC):
                        for g in range(G):
                            last = pe.transpose(b_attn[:, (dc * G + g) * C:(dc * G + g + 1) * C],
                                                x1[:, g, dc * P:(dc + 1) * P], ident[:, :])
                    last.then_inc(x1T_done, 1)

            def z_transposed(p):
                if p.exists():
                    wait(pe, x1T_hi_ready, p.number + 1)
                    wait(pe, x1T_lo_ready, p.number + 1)
                    wait(pe, x1T_copied, p.number + 1)
                    for dc in range(DC):
                        for kc in range(DC):
                            last = three_passes(b_attn[:, dc * G * C:(dc + 1) * G * C],
                                                mT_hi[:, kc, dc * P:(dc + 1) * P], mT_lo[:, kc, dc * P:(dc + 1) * P],
                                                x1T_hi[:, kc, :, :], x1T_lo[:, kc, :, :], kc == 0, kc == DC - 1)
                    last.then_inc(zT_done, 1)

            def values(p):
                if p.exists():
                    wait(pe, x1T_hi_ready, p.number + 1)
                    wait(pe, x1T_lo_ready, p.number + 1)
                    wait(pe, val_copied, p.back(1).number + 1)
                    for g in range(G):
                        for dc in range(DC):
                            last = three_passes(b_val[g][:, 0:D + 2], x1T_hi[:, dc, g, :], x1T_lo[:, dc, g, :],
                                                wvT_hi[:, dc, :], wvT_lo[:, dc, :], dc == 0, dc == DC - 1)
                    last.then_inc(val_done, 1)

            def scores(p):
                if p.exists():
                    wait(pe, x1T_copied, p.number + 1)
                    wait(pe, zT_ready, p.number + 1)
                    for g in range(G):
                        for dc in range(DC):
                            last = pe.matmul(b_attn[:, g * C:(g + 1) * C], zT[:, dc, g, :], x1T[:, dc, g, :],
                                             start=(dc == 0), stop=(dc == DC - 1))
                    last.then_inc(scores_done, 1)

            def attention(p):
                if p.exists():
                    wait(pe, val_copied, p.number + 1)
                    wait(pe, pT_ready, p.number + 1)
                    for g in range(G):
                        wait(pe, pre1_done[g], p.back(-FIRST_AHEAD).clamped + 1)
                        last = pe.matmul(b_att[g][:, 0:D + 2], pT[:, g, :], val[:, g, :], start=True, stop=True)
                    last.then_inc(att_done, 1)

            def iteration(p):
                sh(p.back(2), 1)
                sh(p.back(2), 0)
                x1_transposed(p.back(3))
                attention(p.back(4))
                adj_transposed(p)
                out2(p.back(2), 1)
                out1(p.back(1), 1)
                out1(p.back(1), 0)
                out2(p.back(2), 0)
                node_matrix(p)
                z_transposed(p.back(3))
                values(p.back(3))
                sx(p, 0)
                sx(p, 1)
                scores(p.back(3))

            pe.wait_ge(ident_ready, 1)
            adj_transposed(pair(0))
            w1_transposed()
            pe.wait_ge(consts_set, 4)
            node_matrix(pair(0))
            w2_transposed()
            sx(pair(0), 0)
            sx(pair(0), 1)
            beta_w2()
            pe.wait_ge(w1T_hi_ready, DC)
            pe.wait_ge(w1T_lo_ready, DC)
            iteration(pair(1))
            m_transposed()
            bias_products()
            wv_transposed()
            pe.wait_ge(w2g_hi_ready, 1)
            pe.wait_ge(w2g_lo_ready, 1)
            iteration(pair(2))
            pe.wait_ge(small_ready, 1)
            pe.wait_ge(mT_hi_ready, 1)
            pe.wait_ge(mT_lo_ready, 1)
            pe.wait_ge(wvT_hi_ready, 2)
            pe.wait_ge(wvT_lo_ready, 4)
            over_pairs(pe, iteration, start=3)

        @block.scalar
        def _(act):
            for t, v, landed in ((gamma_col, gamma, gamma_landed), (beta_col, beta, beta_landed)):
                act.dma_start(t[:, :], v.rearrange("(c p) -> p c", p=P),
                              allow_slow_non_contiguous=True).then_inc(landed, 16)

            def split_w1T():
                for dc in range(DC):
                    act.wait_ge(w1T_done, 1 + dc)
                    act.activation(w1T_hi[:, dc, :], b_out1[dc][:, :], ACT.Copy).then_inc(w1T_hi_ready, 1)

            def copy_w2T():
                for j in range(2):
                    act.wait_ge(w2T_done, 1 + j)
                    act.activation(w2T[:, 2 * j:2 * j + 2, :], b_conv2[j][:, :].rearrange("p (c d) -> p c d", c=2),
                                   ACT.Copy).then_inc(w2T_ready, 1)

            def split_w2g():
                act.wait_ge(w2g_ready, HC)
                act.activation(w2g_hi[:, :, :], w2g[:, :, :], ACT.Copy).then_inc(w2g_hi_ready, 1)

            def split_mT():
                act.wait_ge(mT_done, 1)
                act.activation(mT_hi[:, :, :], b_val[0][:, :].rearrange("p (c d) -> p c d", c=DC),
                               ACT.Copy).then_inc(mT_hi_ready, 1)

            def split_wvT():
                act.wait_ge(small_done, 1)
                act.activation(small[:, 0:5], b_attn[:, 0:5], ACT.Copy).then_inc(small_ready, 1)
                act.wait_ge(wvT_done, 1)
                act.activation(wvT_hi[:, :, 0:D], b_val[1][:, :].rearrange("p (c d) -> p c d", c=DC),
                               ACT.Copy).then_inc(wvT_hi_ready, 1)
                act.wait_ge(small_ready, 1)
                act.activation(wvT_hi[:, :, D:D + 1], wkb.unsqueeze(2), ACT.Copy).then_inc(wvT_hi_ready, 1)

            def copy_adjT(p):
                if p.exists():
                    wait(act, pT_ready, p.back(RING).number + 1)
                    wait(act, w_ready, p.back(RING).number + 1)
                    wait(act, adjT_done, p.number + 1)
                    act.activation(adjT[:, p.slot], b_first[:, 0:G * C].rearrange("p (g c) -> p g c", g=G),
                                   ACT.Copy).then_inc(adjT_copied, 1)

            def copy_s(p):
                if p.exists():
                    wait(act, resid_ready, p.back(RING).number + 1)
                    for g in range(G):
                        wait(act, shT_done[g], p.back(RING).number + 1)
                    wait(act, s_done, p.number + 1)
                    act.activation(s_mat[:, p.slot], b_first[:, 0:G * (C + 2)].rearrange("p (g c) -> p g c", g=G),
                                   ACT.Copy).then_inc(s_copied, 1)

            def split_sx(p):
                if p.exists():
                    for g in range(G):
                        wait(act, out1_done[g], p.back(1).number + 1)
                        wait(act, sx_done[g], p.number + 1)
                    act.activation(sx_hi[:, :, :, :], b_first[:, :].rearrange("p (g c n) -> p g c n", g=G, c=DC),
                                   ACT.Copy).then_inc(sx_hi_ready, 1)

            def relu(p, g):
                if p.exists():
                    wait(act, h_ready[g], p.back(1).number + 1)
                    wait(act, pre1_done[g], p.number + 1)
                    act.activation(h_relu[:, g, :], h_pre[:, g, :], ACT.Relu).then_inc(relu_done[g], 1)

            def normalise_h(p, g):
                if p.exists():
                    wait(act, shT_done[g], p.back(1).number + 1)
                    wait(act, rstd1, p.number + 1)
                    wait(act, shift1, p.number + 1)
                    act.activation(h_norm[:, g, :], h_relu[:, g, :], ACT.Identity, scale=ln1_rstd[:, g:g + 1],
                                   bias=ln1_shift[:, g:g + 1]).then_inc(h_ready[g], 1)

            def split_sh(p, g):
                if p.exists():
                    wait(act, out2_done[g], p.back(1).number + 1)
                    wait(act, shT_done[g], p.number + 1)
                    act.activation(sh_hi[:, g], b_conv2[g][:, :].rearrange("p (c n) -> p c n", c=HC),
                                   ACT.Copy).then_inc(sh_hi_ready[g], 1)

            def split_x1T(p):
                if p.exists():
                    wait(act, zT_done, p.back(1).number + 1)
                    wait(act, val_done, p.back(1).number + 1)
                    wait(act, x1T_done, p.number + 1)
                    act.activation(x1T_hi[:, :, :, :], b_attn[:, :].rearrange("p (c g n) -> p c g n", c=DC, g=G),
                                   ACT.Copy).then_inc(x1T_hi_ready, 1)

            def copy_x1T(p):
                if p.exists():
                    wait(act, scores_done, p.back(1).number + 1)
                    wait(act, x1T_lo_ready, p.number + 1)
                    act.activation(x1T[:, :, :, :], b_attn[:, :].rearrange("p (c g n) -> p c g n", c=DC, g=G),
                                   ACT.Copy).then_inc(x1T_copied, 1)

            def copy_zT(p):
                if p.exists():
                    wait(act, scores_done, p.back(1).number + 1)
                    wait(act, zT_done, p.number + 1)
                    for dc in range(DC):
                        last = act.activation(zT[:, dc].rearrange("p g n -> p (g n)"),
                                              b_attn[:, dc * G * C:(dc + 1) * G * C], ACT.Identity,
                                              bias=c2_col[:, dc:dc + 1])
                    last.then_inc(zT_ready, 1)

            def copy_values(p):
                if p.exists():
                    wait(act, att_done, p.back(1).number + 1)
                    wait(act, val_done, p.number + 1)
                    for g in range(G):
                        last = act.activation(val[:, g, 0:D + 1], b_val[g][:, 0:D + 1], ACT.Copy)
                    last.then_inc(val_copied, 1)

            def exponential(p):
                if p.exists():
                    wait(act, pT_ready, p.back(1).number + 1)
                    wait(act, r_ready, p.number + 1)
                    wait(act, scores_done, p.number + 1)
                    for g in range(G):
                        last = act.activation(e_mat[:, g, :], b_attn[:, g * C:(g + 1) * C], ACT.Exp,
                                              bias=r_bias[:, g:g + 1])
                    last.then_inc(exp_done, 1)

            def normalise_y(p):
                if p.exists():
                    wait(act, rstd3, p.number + 1)
                    slot = p.slot % Y_RING
                    wait(act, y_stored[slot], 16 * p.lap * (RING // Y_RING) + 16 * (p.slot // Y_RING))
                    wait(act, shift3, p.number + 1)
                    for g in range(G):
                        last = act.activation(y[:, slot, g, :], y_pre[:, g, :], ACT.Identity, scale=ln3_rstd[:, g:g + 1],
                                              bias=ln3_shift[:, g:g + 1])
                    last.then_inc(y_ready, 1)

            def iteration(p):
                normalise_h(p.back(2), 1)
                normalise_h(p.back(2), 0)
                exponential(p.back(4))
                split_sx(p.back(1))
                split_sh(p.back(2), 1)
                normalise_y(p.back(5))
                split_sh(p.back(2), 0)
                copy_adjT(p)
                split_x1T(p.back(3))
                relu(p.back(1), 1)
                copy_x1T(p.back(3))
                relu(p.back(1), 0)
                copy_s(p)
                copy_zT(p.back(3))
                copy_values(p.back(3))

            copy_adjT(pair(0))
            split_w1T()
            copy_s(pair(0))
            copy_w2T()
            split_sx(pair(0))
            split_w2g()
            copy_adjT(pair(1))
            relu(pair(0), 1)
            copy_s(pair(1))
            relu(pair(0), 0)
            normalise_h(pair(0), 1)
            normalise_h(pair(0), 0)
            split_sx(pair(1))
            split_sh(pair(0), 1)
            split_sh(pair(0), 0)
            copy_adjT(pair(2))
            split_mT()
            split_wvT()
            relu(pair(1), 1)
            relu(pair(1), 0)
            copy_s(pair(2))
            over_pairs(act, iteration, start=3, end=PAIRS + 2)
            exponential(pair(PAIRS - 2))
            split_x1T(pair(PAIRS - 1))
            copy_x1T(pair(PAIRS - 1))
            normalise_y(pair(PAIRS - 3))
            copy_zT(pair(PAIRS - 1))
            copy_values(pair(PAIRS - 1))
            iteration(pair(PAIRS + 3))
            iteration(pair(PAIRS + 4))

        @block.vector
        def _(dve):
            def split_w1T():
                for dc in range(DC):
                    dve.wait_ge(w1T_hi_ready, 1 + dc)
                    dve.tensor_tensor(w1T_lo[:, dc, :], b_out1[dc][:, :], w1T_hi[:, dc, :].bitcast(F32),
                                      ALU.subtract).then_inc(w1T_lo_ready, 1)

            def scale_w2T():
                dve.wait_ge(gamma_landed, 16)
                for hc in range(HC):
                    dve.wait_ge(w2T_ready, 1 + hc // 2)
                    dve.tensor_scalar(w2g[:, hc, :], w2T[:, hc, :], gamma_col[:, hc:hc + 1], 0.5, ALU.mult,
                                      ALU.mult).then_inc(w2g_ready, 1)

            def split_w2g():
                dve.wait_ge(w2g_ready, HC)
                dve.wait_ge(w2g_hi_ready, 1)
                dve.tensor_tensor(w2g_lo[:, :, :], w2g[:, :, :], w2g_hi[:, :, :].bitcast(F32),
                                  ALU.subtract).then_inc(w2g_lo_ready, 1)

            def halve_beta_w2():
                dve.wait_ge(bw2_done, 1)
                dve.tensor_scalar(bw2_half[:, :], b_attn[:, 0:D], 0.5, None, ALU.mult).then_inc(bw2_ready, 1)

            def halve_b2():
                dve.wait_ge(b2_landed, 16)
                dve.tensor_scalar(b2_half[:, :], b2_half[:, :], 0.5, None, ALU.mult).then_inc(b2_halved, 1)

            def split_mT():
                dve.wait_ge(mT_hi_ready, 1)
                dve.tensor_tensor(mT_lo[:, :, :], b_val[0][:, :].rearrange("p (c d) -> p c d", c=DC),
                                  mT_hi[:, :, :].bitcast(F32), ALU.subtract).then_inc(mT_lo_ready, 1)

            def split_wvT():
                dve.wait_ge(wvT_hi_ready, 1)
                dve.tensor_tensor(wvT_lo[:, :, 0:D], b_val[1][:, :].rearrange("p (c d) -> p c d", c=DC),
                                  wvT_hi[:, :, 0:D].bitcast(F32), ALU.subtract).then_inc(wvT_lo_ready, 1)
                dve.wait_ge(wvT_hi_ready, 2)
                dve.tensor_tensor(wvT_lo[:, :, D:D + 1], wkb.unsqueeze(2), wvT_hi[:, :, D:D + 1].bitcast(F32),
                                  ALU.subtract).then_inc(wvT_lo_ready, 1)
                dve.wait_ge(consts_set, 4)
                for t in (wvT_hi, wvT_lo):
                    dve.tensor_copy(t[:, :, D + 1:D + 2], zero_row[:, :].unsqueeze(2)).then_inc(wvT_lo_ready, 1)

            def incidence(p):
                if p.exists():
                    wait(dve, s_done, p.back(1).number + 1)
                    wait(dve, hb_ready, p.back(1).number + 1)
                    wait(dve, adjT_copied, p.number + 1)
                    for g in range(G):
                        dve.tensor_scalar(hT[:, g, :], adjT[:, p.slot, g, :], 0.0, None, ALU.not_equal, ALU.add,
                                          accum_out=count[:, g:g + 1]).then_inc(hT_ready[g], 1)
                    for g in range(G):
                        wait(dve, hT_ready[g], p.number + 1)
                    dve.tensor_scalar(be[:, :], count[:, :], 1.0, None, ALU.max).then_inc(be_clamped, 1)
                    wait(dve, be_clamped, p.number + 1)
                    dve.reciprocal(be[:, :], be[:, :]).then_inc(be_ready, 1)

            def node_weights(p):
                if p.exists():
                    wait(dve, s_copied, p.number + 1)
                    sums = s_mat[:, p.slot, :, C]
                    dve.tensor_scalar(dn_safe[:, :], sums, TINY, None, ALU.max).then_inc(dn_clamped, 1)
                    wait(dve, resid_ready, p.back(RING).number + 1)
                    wait(dve, dn_clamped, p.number + 1)
                    dve.reciprocal(dn_rec[:, :], dn_safe[:, :]).then_inc(dn_inverted, 1)
                    wait(dve, dn_inverted, p.number + 1)
                    dve.scalar_tensor_tensor(dn[:, p.slot, :], sums, 0.0, dn_rec[:, :], ALU.is_gt,
                                             ALU.mult).then_inc(dn_ready, 1)

            ln1 = (h_relu, relu_done, ln1_stats, stats1, ln1_mv, mv1, ln1_ve, ve1, EPS, rstd1)
            ln2 = (u, u_ready, ln2_stats, stats2, ln2_mv, mv2, ln2_ve, ve2, EPS / 4, rstd2)
            ln3 = (y_pre, y_pre_ready, ln3_stats, stats3, ln3_mv, mv3, ln3_ve, ve3, EPS, shift3)

            def statistics(p, ln, g):
                src, src_ready, stats, stats_done = ln[:4]
                if p.exists():
                    wait(dve, src_ready[g], p.number + 1)
                    dve.bn_stats(stats[:, g, :], src[:, g, :]).then_inc(stats_done[g], 1)

            def moments_can_start(p, ln):
                stats_done, taken = ln[3], ln[9]
                if p.exists():
                    wait(dve, taken, p.number)
                    for g in range(G):
                        wait(dve, stats_done[g], p.number + 1)

            def moments(p, ln):
                stats, mv, mv_done, ve, ve_done, eps = ln[2], ln[4], ln[5], ln[6], ln[7], ln[8]
                if p.exists():
                    for g in range(G):
                        last = dve.bn_aggr(mv[:, g, :], stats[:, g, :])
                    last.then_inc(mv_done, 1)
                    wait(dve, mv_done, p.number + 1)
                    dve.tensor_scalar(ve[:, :], mv[:, :, 1], eps, None, ALU.add).then_inc(ve_done, 1)

            def split_sx(p):
                if p.exists():
                    for g in range(G):
                        wait(dve, out1_done[g], p.back(1).number + 1)
                    wait(dve, sx_hi_ready, p.number + 1)
                    dve.tensor_tensor(sx_lo[:, :, :, :], b_first[:, :].rearrange("p (g c n) -> p g c n", g=G, c=DC),
                                      sx_hi[:, :, :, :].bitcast(F32), ALU.subtract).then_inc(sx_lo_ready, 1)

            def first_conv(p, g):
                if p.exists():
                    wait(dve, dn_ready, p.number + 1)
                    wait(dve, relu_done[g], p.back(1).number + 1)
                    wait(dve, out1_done[g], p.number + 1)
                    dve.scalar_tensor_tensor(h_pre[:, g, :], b_out1[g][:, :], dn[:, p.slot, g:g + 1], b1_rows[:, :],
                                             ALU.mult, ALU.add).then_inc(pre1_done[g], 1)

            def shift_h(p):
                if p.exists():
                    for g in range(G):
                        wait(dve, h_ready[g], p.back(1).number + 1)
                    wait(dve, rstd1, p.number + 1)
                    dve.scalar_tensor_tensor(ln1_shift[:, :], ln1_mv[:, :, 0], -1.0, ln1_rstd[:, :], ALU.mult,
                                             ALU.mult).then_inc(shift1, 1)

            def split_sh(p, g):
                if p.exists():
                    wait(dve, out2_done[g], p.back(1).number + 1)
                    wait(dve, sh_hi_ready[g], p.number + 1)
                    dve.tensor_tensor(sh_lo[:, g], b_conv2[g][:, :].rearrange("p (c n) -> p c n", c=HC),
                                      sh_hi[:, g].bitcast(F32), ALU.subtract).then_inc(sh_lo_ready[g], 1)

            def second_conv(p, g):
                if p.exists():
                    wait(dve, resid_ready, p.number + 1)
                    wait(dve, x1_ready, p.back(1).number + 1)
                    wait(dve, out2_done[g], p.number + 1)
                    dve.scalar_tensor_tensor(u[:, g, :], b_conv2[g][:, 0:D], dn[:, p.slot, g:g + 1],
                                             resid[:, p.slot, g, :], ALU.mult, ALU.add).then_inc(u_ready[g], 1)

            def normalise_x1(p):
                if p.exists():
                    wait(dve, x1T_done, p.back(1).number + 1)
                    wait(dve, x1_bv_ready, p.back(1).number + 1)
                    wait(dve, rstd2, p.number + 1)
                    for g in range(G):
                        last = dve.tensor_scalar(x1[:, g, :], u[:, g, :], ln2_mv[:, g, 0:1], ln2_rstd[:, g:g + 1],
                                                 ALU.subtract, ALU.mult)
                    last.then_inc(x1_ready, 1)

            def split_x1T(p):
                if p.exists():
                    wait(dve, zT_done, p.back(1).number + 1)
                    wait(dve, val_done, p.back(1).number + 1)
                    wait(dve, x1T_hi_ready, p.number + 1)
                    dve.tensor_tensor(x1T_lo[:, :, :, :], b_attn[:, :].rearrange("p (c g n) -> p c g n", c=DC, g=G),
                                      x1T_hi[:, :, :, :].bitcast(F32), ALU.subtract).then_inc(x1T_lo_ready, 1)

            def score_bias(p):
                if p.exists():
                    wait(dve, exp_done, p.back(1).number + 1)
                    wait(dve, val_copied, p.number + 1)
                    dve.tensor_scalar(r_bias[:, :], val[:, :, D], bqbk, None, ALU.add).then_inc(r_ready, 1)

            def attention(p):
                if p.exists():
                    wait(dve, att_done, p.number + 1)
                    for g in range(G):
                        dve.reciprocal(den_rec[:, g:g + 1], b_att[g][:, D + 1:D + 2]).then_inc(den_ready[g], 1)
                    wait(dve, x1_bv_ready, p.number + 1)
                    wait(dve, y_ready, p.back(1).number + 1)
                    for g in range(G):
                        wait(dve, den_ready[g], p.number + 1)
                        dve.scalar_tensor_tensor(y_pre[:, g, :], b_att[g][:, 0:D], den_rec[:, g:g + 1], x1_bv[:, g, :],
                                                 ALU.mult, ALU.add).then_inc(y_pre_ready[g], 1)

            def iteration(p):
                statistics(p.back(2), ln1, 1)
                second_conv(p.back(3), 0)
                statistics(p.back(2), ln1, 0)
                moments_can_start(p.back(2), ln1)
                statistics(p.back(3), ln2, 1)
                moments(p.back(2), ln1)
                statistics(p.back(3), ln2, 0)
                statistics(p.back(5), ln3, 0)
                statistics(p.back(5), ln3, 1)
                moments_can_start(p.back(3), ln2)
                shift_h(p.back(2))
                moments(p.back(3), ln2)
                moments_can_start(p.back(5), ln3)
                score_bias(p.back(4))
                moments(p.back(5), ln3)
                node_weights(p.back(1))
                normalise_x1(p.back(3))
                split_sx(p.back(1))
                split_sh(p.back(2), 1)
                attention(p.back(4))
                incidence(p)
                split_sh(p.back(2), 0)
                split_x1T(p.back(3))
                first_conv(p.back(1), 1)
                second_conv(p.back(2), 1)
                first_conv(p.back(1), 0)

            incidence(pair(0))
            split_w1T()
            scale_w2T()
            node_weights(pair(0))
            split_sx(pair(0))
            split_w2g()
            halve_beta_w2()
            incidence(pair(1))
            dve.wait_ge(b1_landed, 16)
            first_conv(pair(0), 1)
            first_conv(pair(0), 0)
            statistics(pair(0), ln1, 1)
            statistics(pair(0), ln1, 0)
            moments_can_start(pair(0), ln1)
            node_weights(pair(1))
            moments(pair(0), ln1)
            halve_b2()
            shift_h(pair(0))
            split_sx(pair(1))
            split_sh(pair(0), 1)
            split_sh(pair(0), 0)
            incidence(pair(2))
            split_mT()
            split_wvT()
            first_conv(pair(1), 1)
            second_conv(pair(0), 1)
            first_conv(pair(1), 0)
            over_pairs(dve, iteration, start=3, end=PAIRS + 2)
            second_conv(pair(PAIRS - 1), 0)
            statistics(pair(PAIRS - 1), ln2, 1)
            statistics(pair(PAIRS - 1), ln2, 0)
            moments_can_start(pair(PAIRS - 1), ln2)
            moments(pair(PAIRS - 1), ln2)
            statistics(pair(PAIRS - 3), ln3, 0)
            statistics(pair(PAIRS - 3), ln3, 1)
            normalise_x1(pair(PAIRS - 1))
            score_bias(pair(PAIRS - 2))
            moments_can_start(pair(PAIRS - 3), ln3)
            moments(pair(PAIRS - 3), ln3)
            split_x1T(pair(PAIRS - 1))
            attention(pair(PAIRS - 2))
            iteration(pair(PAIRS + 3))
            iteration(pair(PAIRS + 4))

        @block.gpsimd
        def _(pool):
            pool.memset(ident[:, :], 0.0).then_inc(ident_zeroed, 1)
            pool.wait_ge(ident_zeroed, 1)
            pool.affine_select(out=ident[:, :], in_=ident[:, :], compare_op=ALU.not_equal, fill=1.0, base=0,
                               pattern=[[-1, P]], channel_multiplier=1).then_inc(ident_ready, 1)
            pool.memset(neg_half[:, :], -0.5).then_inc(consts_set, 1)
            pool.memset(zero_row[:, :], 0.0).then_inc(consts_set, 1)
            pool.memset(val[:, :, D + 1:D + 2], 1.0).then_inc(consts_set, 1)
            pool.memset(hb[:, :, C + 1:C + 2], 1.0).then_inc(consts_set, 1)
            for t, v in ((bq_col, wq_b), (bk_col, wk_b)):
                pool.dma_start(t[:, :], v.rearrange("(c p) -> p c", p=P),
                               allow_slow_non_contiguous=True).then_inc(bqk_landed, 16)

            def first_row(p):
                if p.exists():
                    wait(pool, s_done, p.back(1).number + 1)
                    wait(pool, adjT_copied, p.number + 1)
                    pool.tensor_tensor(hb[:, :, C:C + 1], adjT[:, p.slot, :, 0:1], zero_row[:, :].unsqueeze(2),
                                       ALU.add).then_inc(w_ready, 1)

            def edge_weights(p):
                if p.exists():
                    wait(pool, s_done, p.back(1).number + 1)
                    for g in range(G):
                        wait(pool, hT_ready[g], p.number + 1)
                    wait(pool, be_ready, p.number + 1)
                    pool.tensor_tensor(hb[:, :, 0:C], hT[:, :, :], be[:, :].unsqueeze(2).to_broadcast([P, G, C]),
                                       ALU.mult).then_inc(hb_ready, 1)

            def rsqrt(p, ve, ve_done, rstd, rstd_done):
                wait(pool, ve_done, p.number + 1)
                pool.tensor_tensor(rstd[:, :], ve[:, :], neg_half[:, :], ALU.pow).then_inc(rstd_done, 1)

            def degree_term(p):
                if p.exists():
                    wait(pool, dn_ready, p.number + 1)
                    pool.tensor_tensor(dn_deg[:, :], dn[:, p.slot, :], s_mat[:, p.slot, :, C + 1],
                                       ALU.mult).then_inc(dn_deg_ready, 1)

            def beta_term_scaled(p):
                if p.exists():
                    wait(pool, dn_deg_ready, p.number + 1)
                    pool.tensor_tensor(beta_term[:, :, :], bw2_half[:, :].unsqueeze(1).to_broadcast([P, G, D]),
                                       dn_deg[:, :].unsqueeze(2).to_broadcast([P, G, D]),
                                       ALU.mult).then_inc(beta_scaled, 1)

            def beta_term_biased(p):
                if p.exists():
                    wait(pool, beta_scaled, p.number + 1)
                    pool.tensor_tensor(beta_term[:, :, :], beta_term[:, :, :],
                                       b2_half[:, :].unsqueeze(1).to_broadcast([P, G, D]),
                                       ALU.add).then_inc(beta_biased, 1)

            def residual(p):
                if p.exists():
                    wait(pool, x_landed[p.slot], p.lap * 16 + 16)
                    for g in range(G):
                        wait(pool, u_ready[g], p.back(RING).number + 1)
                    wait(pool, beta_biased, p.number + 1)
                    pool.tensor_tensor(resid[:, p.slot], x_in[:, p.slot], beta_term[:, :, :],
                                       ALU.add).then_inc(resid_ready, 1)

            def rstd_of_h(p):
                if p.exists():
                    for g in range(G):
                        wait(pool, h_ready[g], p.back(1).number + 1)
                    rsqrt(p, ln1_ve, ve1, ln1_rstd, rstd1)

            def rstd_of_x1(p):
                if p.exists():
                    wait(pool, x1_ready, p.back(1).number + 1)
                    rsqrt(p, ln2_ve, ve2, ln2_rstd, rstd2)

            def rstd_of_y(p):
                if p.exists():
                    wait(pool, y_ready, p.back(1).number + 1)
                    rsqrt(p, ln3_ve, ve3, ln3_rstd, rstd3)
                    pool.tensor_tensor(ln3_neg[:, :], zero_row[:, :], ln3_mv[:, :, 0], ALU.subtract).then_inc(neg3, 1)
                    wait(pool, rstd3, p.number + 1)
                    wait(pool, neg3, p.number + 1)
                    pool.tensor_tensor(ln3_shift[:, :], ln3_neg[:, :], ln3_rstd[:, :], ALU.mult).then_inc(shift3, 1)

            def add_value_bias(p):
                if p.exists():
                    wait(pool, x1_ready, p.number + 1)
                    for g in range(G):
                        wait(pool, y_pre_ready[g], p.back(1).number + 1)
                    pool.tensor_tensor(x1_bv[:, :, :], x1[:, :, :], bv_rows[:, :].unsqueeze(1).to_broadcast([P, G, D]),
                                       ALU.add).then_inc(x1_bv_ready, 1)

            def weigh(p):
                if p.exists():
                    wait(pool, att_done, p.back(1).number + 1)
                    wait(pool, exp_done, p.number + 1)
                    pool.tensor_tensor(pT[:, :, :], adjT[:, p.slot], e_mat[:, :, :], ALU.mult).then_inc(pT_ready, 1)

            def iteration(p):
                beta_term_scaled(p.back(2))
                add_value_bias(p.back(4))
                rstd_of_h(p.back(2))
                rstd_of_x1(p.back(3))
                rstd_of_y(p.back(5))
                weigh(p.back(4))
                first_row(p)
                beta_term_biased(p.back(2))
                residual(p.back(2))
                edge_weights(p)
                degree_term(p.back(1))

            pool.wait_ge(consts_set, 4)
            iteration(pair(0))
            iteration(pair(1))
            pool.wait_ge(bw2_ready, 1)
            pool.wait_ge(b2_halved, 1)
            pool.wait_ge(bv_landed, 16)
            over_pairs(pool, iteration, start=2, end=PAIRS + 2)
            add_value_bias(pair(PAIRS - 2))
            rstd_of_x1(pair(PAIRS - 1))
            weigh(pair(PAIRS - 2))
            rstd_of_y(pair(PAIRS - 3))
            iteration(pair(PAIRS + 3))
            iteration(pair(PAIRS + 4))


_INS = ['x', 'adj', 'L0_gnn_W1', 'L0_gnn_b1', 'L0_gnn_gamma', 'L0_gnn_beta', 'L0_gnn_W2', 'L0_gnn_b2',
        'L1_gnn_Wq_w', 'L1_gnn_Wq_b', 'L1_gnn_Wk_w', 'L1_gnn_Wk_b', 'L1_gnn_Wv_w', 'L1_gnn_Wv_b']


def kernel(**inputs):
    import numpy as _np
    import concourse.bacc as _bacc
    from concourse import mybir as _mybir
    from concourse.bass_utils import run_bass_kernel_spmd as _run

    nc = _bacc.Bacc("TRN2", target_bir_lowering=False, num_devices=1)
    arrays, args = {}, []
    for name in _INS:
        a = _np.ascontiguousarray(inputs[name])
        arrays[f"in_{name}_dram"] = a
        args.append(nc.dram_tensor(f"in_{name}_dram", a.shape, _mybir.dt.from_np(a.dtype), kind="ExternalInput").ap())
    shape = arrays["in_x_dram"].shape
    args.append(nc.dram_tensor("out_dram", shape, _mybir.dt.float32, kind="ExternalOutput").ap())
    build(nc, *args)
    r = _run(nc, [arrays], core_ids=[0])
    return r.results[0]["out_dram"]
```
